# Optimizing a Trainium2 kernel written in Bass

```python
import numpy as np
import jax
import jax.numpy as jnp

def _softmax(x, axis=-1):
    return jax.nn.softmax(x, axis=axis)

def _gelu(x):
    return jax.nn.gelu(x, approximate=True)

def _silu(x):
    return jax.nn.silu(x)

def _sigmoid(x):
    return jax.nn.sigmoid(x)

def _layernorm(x, axis=-1, eps=1e-05):
    m = jnp.mean(x, axis=axis, keepdims=True)
    v = jnp.var(x, axis=axis, keepdims=True)
    return (x - m) / jnp.sqrt(v + eps)

def _scatter_add(tgt, idx, src, axis=0):
    return tgt.at[idx].add(src)

def _segment_sum(src, seg, n):
    return jax.ops.segment_sum(src, seg, n)
kernel_name = 'mk_gnn_ffn_d2_gnn_r8_e3a41a'

def setup_inputs(seed: int=0):
    np.random.seed(seed)
    _w = jnp.asarray

    def _rec_inputs():
        import jax
        import jax.numpy as jnp
        _gk = jax.random.key(seed)
        x = -0.0002117 + 1 * jax.random.normal(jax.random.fold_in(_gk, 1), (12500, 256), jnp.float32)
        src = jax.random.randint(jax.random.fold_in(_gk, 2), (200000,), 0, 12500, jnp.int32)
        dst = jnp.minimum((12500 * jax.random.uniform(jax.random.fold_in(_gk, 3), (200000,)) ** 2.0).astype(jnp.int32), 99999)
        _o = jnp.argsort(dst, stable=True)
        src = src[_o]
        dst = dst[_o]
        edge_weight = jax.random.uniform(jax.random.fold_in(_gk, 12), (200000,), jnp.float32, 0.0, 1)
        return (x, src, dst, edge_weight)
    x, src, dst, edge_weight = _rec_inputs()

    def _L0_gnn_setup():
        import jax, jax.numpy as jnp
        import numpy as np
        N = 12500
        E = 400000
        IN = 256
        OUT = 256
        L = 4
        D = OUT // L
        key = jax.random.key(seed)
        ks = jax.random.split(key, 8)
        return {'x': jax.random.normal(ks[0], (N, IN), jnp.float32), 'src': jax.random.randint(ks[1], (E,), 0, N, jnp.int32), 'dst': jax.random.randint(ks[2], (E,), 0, N, jnp.int32), 'W_lin': jax.random.normal(ks[3], (IN, OUT), jnp.float32) * (1.0 / np.sqrt(IN)), 'b_lin': jnp.zeros((OUT,), jnp.float32), 'att_w': jax.random.normal(ks[4], (L, 2 * OUT), jnp.float32) * (1.0 / np.sqrt(2 * OUT)), 'att_b': jnp.zeros((L,), jnp.float32), 'emb_w': jax.random.normal(ks[5], (IN, D), jnp.float32) * (1.0 / np.sqrt(IN)), 'emb_b': jnp.zeros((D,), jnp.float32)}
    _L0_gnn_all = _L0_gnn_setup()
    _L0_gnn_in = {k: v for k, v in _L0_gnn_all.items() if k in ('W_lin', 'b_lin', 'att_w', 'att_b', 'emb_w', 'emb_b')}
    del _L0_gnn_all

    def _L0_ffn_setup():
        import jax, jax.numpy as jnp
        import numpy as np
        B, A = (512, 8)
        IN, OUT = (256, 256)
        SH1, SH2 = (256, 128)
        EH1, EH2 = (128, 64)
        E, TOPK = (4, 2)

        def _shared_mlp(x, W1, b1, W2, b2, W3, b3):
            h = jax.nn.relu(x @ W1 + b1)
            h = jax.nn.relu(h @ W2 + b2)
            return h @ W3 + b3

        def _experts_mlp(x, eW1, eb1, eW2, eb2, eW3, eb3):
            h = jax.nn.relu(jnp.einsum('baf,efh->ebah', x, eW1) + eb1[:, None, None, :])
            h = jax.nn.relu(jnp.einsum('ebah,ehg->ebag', h, eW2) + eb2[:, None, None, :])
            o = jnp.einsum('ebag,ego->ebao', h, eW3) + eb3[:, None, None, :]
            return jnp.moveaxis(o, 0, -1)
        key = jax.random.key(seed)
        ks = jax.random.split(key, 16)
        s = 0.05
        return {'x': jax.random.normal(ks[0], (B, A, IN), jnp.float32), 'sW1': jax.random.normal(ks[1], (IN, SH1), jnp.float32) * s, 'sb1': jnp.zeros((SH1,), jnp.float32), 'sW2': jax.random.normal(ks[2], (SH1, SH2), jnp.float32) * s, 'sb2': jnp.zeros((SH2,), jnp.float32), 'sW3': jax.random.normal(ks[3], (SH2, OUT), jnp.float32) * s, 'sb3': jnp.zeros((OUT,), jnp.float32), 'eW1': jax.random.normal(ks[4], (E, IN, EH1), jnp.float32) * s, 'eb1': jnp.zeros((E, EH1), jnp.float32), 'eW2': jax.random.normal(ks[5], (E, EH1, EH2), jnp.float32) * s, 'eb2': jnp.zeros((E, EH2), jnp.float32), 'eW3': jax.random.normal(ks[6], (E, EH2, OUT), jnp.float32) * s, 'eb3': jnp.zeros((E, OUT), jnp.float32), 'gW': jax.random.normal(ks[7], (IN, E), jnp.float32) * s, 'gb': jnp.zeros((E,), jnp.float32)}
    _L0_ffn_all = _L0_ffn_setup()
    _L0_ffn_in = {k: v for k, v in _L0_ffn_all.items() if k in ('sW1', 'sb1', 'sW2', 'sb2', 'sW3', 'sb3', 'eW1', 'eb1', 'eW2', 'eb2', 'eW3', 'eb3', 'gW', 'gb')}
    del _L0_ffn_all

    def _L1_gnn_setup():
        import jax, jax.numpy as jnp
        import numpy as np
        N_NODES = 12500
        N_RAND_EDGES = 412500
        D = 256
        key = jax.random.key(seed)
        k1, k2, k3, k4 = jax.random.split(key, 4)
        feats = jax.random.normal(k1, (N_NODES, D), dtype=jnp.float32)
        rows = jnp.concatenate([jax.random.randint(k2, (N_RAND_EDGES,), 0, N_NODES, dtype=jnp.int32), jnp.arange(N_NODES, dtype=jnp.int32)])
        cols = jnp.concatenate([jax.random.randint(k3, (N_RAND_EDGES,), 0, N_NODES, dtype=jnp.int32), jnp.arange(N_NODES, dtype=jnp.int32)])
        vals = jnp.ones((N_RAND_EDGES + N_NODES,), dtype=jnp.float32)
        limit = float(np.sqrt(6.0 / (D + D)))
        W = jax.random.uniform(k4, (D, D), dtype=jnp.float32, minval=-limit, maxval=limit)
        b = jnp.zeros((D,), dtype=jnp.float32)
        return {'feats': feats, 'rows': rows, 'cols': cols, 'vals': vals, 'W': W, 'b': b}
    _L1_gnn_all = _L1_gnn_setup()
    _L1_gnn_in = {k: v for k, v in _L1_gnn_all.items() if k in ('W', 'b')}
    del _L1_gnn_all

    def _L1_ffn_setup():
        import jax, jax.numpy as jnp
        import numpy as np
        B, S, D = (8, 512, 256)
        H = 4 * D
        CAPACITY = 0.5
        key = jax.random.key(seed)
        ks = jax.random.split(key, 6)
        x = jax.random.normal(ks[0], (B, S, D), dtype=jnp.float32)
        attention_mask = jnp.zeros((B, 1, 1, S), dtype=jnp.float32)
        wr = jax.random.normal(ks[1], (D, 1), dtype=jnp.float32) * 0.02
        br = jnp.zeros((1,), dtype=jnp.float32)
        w1 = jax.random.normal(ks[2], (D, H), dtype=jnp.float32) * 0.02
        b1 = jnp.zeros((H,), dtype=jnp.float32)
        w2 = jax.random.normal(ks[3], (H, D), dtype=jnp.float32) * 0.02
        b2 = jnp.zeros((D,), dtype=jnp.float32)
        return {'x': x, 'attention_mask': attention_mask, 'wr': wr, 'br': br, 'w1': w1, 'b1': b1, 'w2': w2, 'b2': b2}
    _L1_ffn_all = _L1_ffn_setup()
    _L1_ffn_in = {k: v for k, v in _L1_ffn_all.items() if k in ('attention_mask', 'wr', 'br', 'w1', 'b1', 'w2', 'b2')}
    del _L1_ffn_all
    return {'x': x, 'src': src, 'dst': dst, 'edge_weight': edge_weight, 'L0_gnn_W_lin': _L0_gnn_in['W_lin'], 'L0_gnn_b_lin': _L0_gnn_in['b_lin'], 'L0_gnn_att_w': _L0_gnn_in['att_w'], 'L0_gnn_att_b': _L0_gnn_in['att_b'], 'L0_gnn_emb_w': _L0_gnn_in['emb_w'], 'L0_gnn_emb_b': _L0_gnn_in['emb_b'], 'L0_ffn_sW1': _L0_ffn_in['sW1'], 'L0_ffn_sb1': _L0_ffn_in['sb1'], 'L0_ffn_sW2': _L0_ffn_in['sW2'], 'L0_ffn_sb2': _L0_ffn_in['sb2'], 'L0_ffn_sW3': _L0_ffn_in['sW3'], 'L0_ffn_sb3': _L0_ffn_in['sb3'], 'L0_ffn_eW1': _L0_ffn_in['eW1'], 'L0_ffn_eb1': _L0_ffn_in['eb1'], 'L0_ffn_eW2': _L0_ffn_in['eW2'], 'L0_ffn_eb2': _L0_ffn_in['eb2'], 'L0_ffn_eW3': _L0_ffn_in['eW3'], 'L0_ffn_eb3': _L0_ffn_in['eb3'], 'L0_ffn_gW': _L0_ffn_in['gW'], 'L0_ffn_gb': _L0_ffn_in['gb'], 'L1_gnn_W': _L1_gnn_in['W'], 'L1_gnn_b': _L1_gnn_in['b'], 'L1_ffn_attention_mask': _L1_ffn_in['attention_mask'], 'L1_ffn_wr': _L1_ffn_in['wr'], 'L1_ffn_br': _L1_ffn_in['br'], 'L1_ffn_w1': _L1_ffn_in['w1'], 'L1_ffn_b1': _L1_ffn_in['b1'], 'L1_ffn_w2': _L1_ffn_in['w2'], 'L1_ffn_b2': _L1_ffn_in['b2']}

def reference(x, src, dst, edge_weight, L0_gnn_W_lin, L0_gnn_b_lin, L0_gnn_att_w, L0_gnn_att_b, L0_gnn_emb_w, L0_gnn_emb_b, L0_ffn_sW1, L0_ffn_sb1, L0_ffn_sW2, L0_ffn_sb2, L0_ffn_sW3, L0_ffn_sb3, L0_ffn_eW1, L0_ffn_eb1, L0_ffn_eW2, L0_ffn_eb2, L0_ffn_eW3, L0_ffn_eb3, L0_ffn_gW, L0_ffn_gb, L1_gnn_W, L1_gnn_b, L1_ffn_attention_mask, L1_ffn_wr, L1_ffn_br, L1_ffn_w1, L1_ffn_b1, L1_ffn_w2, L1_ffn_b2):
    import jax
    import jax.numpy as jnp

    def _L0_gnn_ref(x, src, dst, W_lin, b_lin, att_w, att_b, emb_w, emb_b):
        import jax, jax.numpy as jnp
        import numpy as np
        N = 12500
        E = 400000
        IN = 256
        OUT = 256
        L = 4
        D = OUT // L
        n = x.shape[0]
        h = x @ W_lin + b_lin
        h_em = x @ emb_w + emb_b
        out_dim = h.shape[1]
        a_src = att_w[:, :out_dim]
        a_dst = att_w[:, out_dim:]
        s_src = h @ a_src.T
        s_dst = h @ a_dst.T
        e_ob = jax.nn.sigmoid(s_src[src] + s_dst[dst] + att_b)
        ev = jnp.exp(e_ob - jnp.max(e_ob, axis=0, keepdims=True))
        denom = jax.ops.segment_sum(ev, src, num_segments=n)
        attn = ev / denom[src]
        h_em_dst = h_em[dst]
        heads = [jax.ops.segment_sum(attn[:, l:l + 1] * h_em_dst, src, num_segments=n) for l in range(att_w.shape[0])]
        return jnp.concatenate(heads, axis=-1)

    def _L0_ffn_ref(x, sW1, sb1, sW2, sb2, sW3, sb3, eW1, eb1, eW2, eb2, eW3, eb3, gW, gb):
        import jax, jax.numpy as jnp
        import numpy as np
        B, A = (512, 8)
        IN, OUT = (256, 256)
        SH1, SH2 = (256, 128)
        EH1, EH2 = (128, 64)
        E, TOPK = (4, 2)

        def _shared_mlp(x, W1, b1, W2, b2, W3, b3):
            h = jax.nn.relu(x @ W1 + b1)
            h = jax.nn.relu(h @ W2 + b2)
            return h @ W3 + b3

        def _experts_mlp(x, eW1, eb1, eW2, eb2, eW3, eb3):
            h = jax.nn.relu(jnp.einsum('baf,efh->ebah', x, eW1) + eb1[:, None, None, :])
            h = jax.nn.relu(jnp.einsum('ebah,ehg->ebag', h, eW2) + eb2[:, None, None, :])
            o = jnp.einsum('ebag,ego->ebao', h, eW3) + eb3[:, None, None, :]
            return jnp.moveaxis(o, 0, -1)
        all_out = _experts_mlp(x, eW1, eb1, eW2, eb2, eW3, eb3)
        shared = _shared_mlp(x, sW1, sb1, sW2, sb2, sW3, sb3)
        gates = jax.nn.softmax(x @ gW + gb, axis=-1)
        topv, topi = jax.lax.top_k(gates, TOPK)
        topw = jax.nn.softmax(topv, axis=-1)
        sel = jnp.take_along_axis(all_out, topi[:, :, None, :], axis=-1)
        gated = jnp.sum(sel * topw[:, :, None, :], axis=-1)
        return shared + gated

    def _L1_gnn_ref(feats, rows, cols, vals, W, b):
        import jax, jax.numpy as jnp
        import numpy as np
        N_NODES = 12500
        N_RAND_EDGES = 412500
        D = 256
        msgs = vals[:, None] * feats[cols]
        agg = jax.ops.segment_sum(msgs, rows, num_segments=feats.shape[0])
        degree = jax.ops.segment_sum(vals, rows, num_segments=feats.shape[0])
        to_feats = agg / degree[:, None]
        to_feats = jax.nn.relu(to_feats @ W.T + b)
        return feats + to_feats

    def _L1_ffn_ref(x, attention_mask, wr, br, w1, b1, w2, b2):
        import jax, jax.numpy as jnp
        import numpy as np
        B, S, D = (8, 512, 256)
        H = 4 * D
        CAPACITY = 0.5
        b, s, d = x.shape
        weights = (jnp.einsum('bsd,do->bso', x, wr) + br)[..., 0]
        k = max(1, int(CAPACITY * s))
        kk = k - 1 if k > 1 else 1
        _, idx = jax.lax.top_k(weights, k)
        sel_idx = idx[:, :kk]
        sel = jnp.take_along_axis(x, sel_idx[:, :, None], axis=1)
        h = jax.nn.gelu(jnp.einsum('bkd,dh->bkh', sel, w1) + b1)
        y = jnp.einsum('bkh,hd->bkd', h, w2) + b2
        w_sel = jnp.take_along_axis(weights, sel_idx, axis=1)
        y = y * w_sel[..., None]
        batch_idx = jnp.arange(b)[:, None]
        processed = jnp.zeros_like(x).at[batch_idx, sel_idx].set(y)
        return processed + x
    x = x + _L0_gnn_ref(_layernorm(x, axis=-1), src, dst, L0_gnn_W_lin, L0_gnn_b_lin, L0_gnn_att_w, L0_gnn_att_b, L0_gnn_emb_w, L0_gnn_emb_b)
    x = x + _L0_ffn_ref(_layernorm(x, axis=-1)[None], L0_ffn_sW1, L0_ffn_sb1, L0_ffn_sW2, L0_ffn_sb2, L0_ffn_sW3, L0_ffn_sb3, L0_ffn_eW1, L0_ffn_eb1, L0_ffn_eW2, L0_ffn_eb2, L0_ffn_eW3, L0_ffn_eb3, L0_ffn_gW, L0_ffn_gb)[0]
    x = x + _L1_gnn_ref(_layernorm(x, axis=-1), src, dst, edge_weight, L1_gnn_W, L1_gnn_b)
    x = x + _L1_ffn_ref(_layernorm(x, axis=-1)[None], L1_ffn_attention_mask, L1_ffn_wr, L1_ffn_br, L1_ffn_w1, L1_ffn_b1, L1_ffn_w2, L1_ffn_b2)[0]
    return x

_drawn_inputs = setup_inputs


def setup_inputs(seed=0):
    import zlib

    import numpy as np

    out = dict(_drawn_inputs(seed))
    spreads = {'L0_gnn_b_lin': (0.0, 2.0),
     'L0_gnn_att_b': (0.0, 2.0),
     'L0_gnn_emb_b': (0.0, 0.1),
     'L0_ffn_sb1': (0.0, 0.4),
     'L0_ffn_sb2': (0.0, 0.1),
     'L0_ffn_sb3': (0.0, 0.1),
     'L0_ffn_eb1': (0.0, 0.8),
     'L0_ffn_eb2': (0.0, 0.49),
     'L0_ffn_eb3': (0.0, 0.1),
     'L0_ffn_gb': (0.0, 0.366),
     'L1_gnn_b': (0.0, 0.1),
     'L1_ffn_b1': (0.0, 0.8),
     'L1_ffn_b2': (0.0, 0.8)}
    factors = {'L1_ffn_wr': 6.18, 'L1_ffn_w1': 8.0, 'L1_ffn_w2': 7.77}
    for name, (base, spread) in spreads.items():
        noise = np.random.default_rng([zlib.crc32(name.encode()), seed]).standard_normal(out[name].shape)
        drawn = base * np.exp(spread * noise) if base else spread * noise
        out[name] = jnp.asarray(drawn.astype(out[name].dtype))
    for name, factor in factors.items():
        out[name] = (out[name] * factor).astype(out[name].dtype)
    return out
```

```python
import concourse.bass as bass
from concourse import mybir
from contextlib import ExitStack

F32 = mybir.dt.float32
BF16 = mybir.dt.bfloat16
I32 = mybir.dt.int32
U32 = mybir.dt.uint32
ALU = mybir.AluOpType
ACT = mybir.ActivationFunctionType

N, E, D = 12500, 200000, 256
P = 128
HEADS, HD = 4, 64
ROW0 = HD + HEADS
MSG0 = HEADS * HD + HEADS
EXPERTS = 4
HID = 1024
BLK = HID // P
LN_EPS = 1e-5
CAPACITY = N // 2 - 1

QUAD = 4
TR = -(-N // P)
T = -(-TR // QUAD) * QUAD
ST = T // QUAD
TOK = QUAD * P
NP = T * P

SLOTS = 16
HALF = SLOTS // 2
EJ = -(-E // (P * SLOTS)) * SLOTS
EH = EJ // 2
PAD_SRC = NP

MIN_PAIRS = 3
PAIR = 2 * P
MAX_PAIRS = E // PAIR + MIN_PAIRS * T
LOOK = 2
RING = SLOTS // 2
CS = 2 * (MAX_PAIRS + LOOK + RING) + -(-(EJ * P - E) // P)
REC = 3

AHEAD = 8
FAR = 32


class Chain:

    def __init__(self, eng, sem, base=0):
        self.eng, self.sem, self.base, self.n = eng, sem, base, 0

    def step(self, ins):
        ins.then_inc(self.sem, 1)
        self.n += 1

    def wait(self):
        self.eng.wait_ge(self.sem, self.base + self.n)

    def wait_apart(self):
        self.wait()
        self.eng.sem_inc(self.sem, 1)
        self.n += 1

    def link(self, ins):
        self.step(ins)
        self.wait()


def flat(ap):
    return ap.rearrange("p a b -> p (a b)")


class Core:

    def __init__(self, nc, ctx, io):
        self.nc, self.ctx, self.io = nc, ctx, io
        sb, dram = self.sb, self.dram
        self.ident_f = sb("ident_f", [P, P])
        self.ident_b = sb("ident_b", [P, P], BF16)
        self.before = sb("before", [P, P], BF16)
        self.not_before = sb("not_before", [P, P], BF16)
        self.ones_f = sb("ones_f", [P, P])
        self.zero_b = sb("zero_b", [1, MSG0 + P], BF16)
        self.iota_f = sb("iota_f", [P, P])
        self.rows = sb("rows", [P, T, D])
        self.recs = sb("recs", [P, CS, REC])
        self.s_src = sb("s_src", [P, T + 1, 3 * HEADS], BF16)
        self.pair_i = sb("pair_i", [P, T + 1], I32)
        self.rounds_i = sb("rounds_i", [P, 1], I32)
        self.base_f = sb("base_f", [P, T + 1])
        self.base2_f = sb("base2_f", [P, T + 1])
        self.score = sb("score", [P, T])
        self.tab0 = dram("tab0", [TR * P, ROW0])
        self.tab1 = dram("tab1", [NP, D])
        self.base3 = dram("base3", [NP, D])
        self.sorted = dram("sorted", [P * CS, REC])

    def sb(self, name, shape, dt=F32, ctx=None):
        return (ctx or self.ctx).enter_context(self.nc.sbuf_tensor(name, shape, dt))

    def ps(self, ctx, name, shape, dt=F32):
        return ctx.enter_context(self.nc.psum_tensor(name, shape, dt))

    def sem(self, ctx, name):
        return ctx.enter_context(self.nc.semaphore(name))

    def dram(self, name, shape):
        return self.nc.dram_tensor(name, shape, F32, kind="Internal").ap()


def rstd_steps(dve, ch, var, y, tmp):
    ch.link(dve.tensor_scalar(var, var, LN_EPS, None, ALU.add))
    ch.link(dve.tensor_scalar(tmp.bitcast(I32), var.bitcast(I32), 1, None, ALU.logical_shift_right))
    ch.link(dve.tensor_scalar(y.bitcast(I32), tmp.bitcast(I32), -1.0, float(0x5F3759DF), ALU.mult, ALU.add))
    for _ in range(3):
        ch.link(dve.tensor_tensor(tmp, y, y, ALU.mult))
        ch.link(dve.scalar_tensor_tensor(tmp, tmp, -0.5, var, ALU.mult, ALU.mult))
        ch.link(dve.scalar_tensor_tensor(y, tmp, 1.5, y, ALU.add, ALU.mult))


class Edges:

    def __init__(self, core):
        words = flat(core.rows[:, :, :])
        part = lambda n: words[:, n * EJ:(n + 1) * EJ]
        self.src, self.dst, self.tmp = part(0).bitcast(I32), part(1).bitcast(I32), part(2).bitcast(I32)
        self.weight, self.row, self.tile, self.junk = part(3), part(4), part(5), part(6)


    def half(self, words, g):
        return words[:, g * EH:(g + 1) * EH]


class Weights:

    def __init__(self, core):
        sb = core.sb
        self.small = sb("w_small", [P, 2, ROW0 + HEADS])
        self.small_bias = sb("w_small_bias", [P, ROW0 + HEADS])
        self.spread = sb("w_spread", [EXPERTS + 1, 2, P])
        self.up1 = sb("w_up1", [P, 2, (2 + EXPERTS) * P])
        self.up1_bias = sb("w_up1_bias", [P, 2 + EXPERTS])
        self.up2 = sb("w_up2", [P, 2, P])
        self.up2_bias = sb("w_up2_bias", [P, 1])
        self.expert2 = sb("w_expert2", [P, EXPERTS, HD])
        self.expert2_bias = sb("w_expert2_bias", [P, 2])
        self.down = sb("w_down", [P, 3, D])
        self.down_bias = sb("w_down_bias", [EXPERTS + 1, D])
        self.gate = sb("w_gate", [P, 2, EXPERTS])
        self.gate_bias = sb("w_gate_bias", [P, EXPERTS])

    def layer0_loads(self, io):
        g = lambda n: io["L0_ffn_" + n]
        col = lambda a: a.rearrange("(b p) -> p b", p=P)
        return [
            (self.up1[:, :, 0:2 * P], g("sW1").rearrange("(k p) n -> p k n", p=P)),
            *[(self.up1[:, :, (2 + e) * P:(3 + e) * P], g("eW1")[e, :, :].rearrange("(k p) n -> p k n", p=P))
              for e in range(EXPERTS)],
            (self.up1_bias[:, 0:2], col(g("sb1"))),
            (self.up1_bias[:, 2:2 + EXPERTS], g("eb1").rearrange("e p -> p e")),
            (self.up2[:, :, :], g("sW2").rearrange("(k p) n -> p k n", p=P)),
            (self.up2_bias[:, :], col(g("sb2"))),
            (self.expert2[:, :, :], g("eW2").rearrange("e p n -> p e n")),
            (self.expert2_bias[:, :], g("eb2").rearrange("(a b) n -> (b n) a", b=2)),
            (self.down[:, 0, :], g("sW3")),
            *[(self.down[:, 1 + a, :], g("eW3")[2 * a:2 * a + 2, :, :].rearrange("b n d -> (b n) d")) for a in range(2)],
            (self.down_bias[0:EXPERTS, :], g("eb3")),
            (self.down_bias[EXPERTS:EXPERTS + 1, :], g("sb3").rearrange("(a n) -> a n", a=1)),
            (self.gate[:, :, :], g("gW").rearrange("(k p) n -> p k n", p=P)),
            (self.gate_bias[:, :], g("gb").partition_broadcast(P)),
        ]


def setup(core, w):
    nc, io = core.nc, core.io
    with ExitStack() as ctx:
        sem = lambda n: core.sem(ctx, n)
        src_loaded, edges_loaded = sem("src_loaded"), sem("edges_loaded")
        lin_loaded, weights_loaded = sem("lin_loaded"), sem("weights_loaded")
        masks, consts_ready, dve_own, act_own = sem("masks"), sem("consts_ready"), sem("dve_own"), sem("act_own")
        cleared, sorted_cleared = sem("cleared"), sem("sorted_cleared")
        hist_ready, totals_ready, lin_t_psum, lin_t_ready = sem("hist_ready"), sem("totals_ready"), sem("lin_t_psum"), sem("lin_t_ready")
        small_psum, bias_row_ready, bias_psum = sem("small_psum"), sem("bias_row_ready"), sem("bias_psum")
        small_ready = sem("small_ready")

        iota_i = core.sb("iota_i", [P, P], I32, ctx)
        hist = core.sb("hist", [P, 2, T + 1], ctx=ctx)
        count = core.sb("count", [P, 2], ctx=ctx)
        npairs = core.sb("npairs", [P, T + 1], ctx=ctx)
        npairs_i = core.sb("npairs_i", [P, T + 1], I32, ctx)
        first_pair = core.sb("first_pair", [P, T + 1], ctx=ctx)
        zeros = core.sb("zeros", [P, T + 1], ctx=ctx)
        lin = core.sb("lin", [P, 2, D], ctx=ctx)
        lin_t = core.sb("lin_t", [P, 2, D], ctx=ctx)
        att = core.sb("att", [HEADS, 2 * D], ctx=ctx)
        att_t = core.sb("att_t", [P, 4, HEADS], ctx=ctx)
        b_lin = core.sb("b_lin", [P, 2], ctx=ctx)
        bias_row = core.sb("bias_row", [1, ROW0 + HEADS], ctx=ctx)
        b_parts = core.sb("b_parts", [1, ROW0], ctx=ctx)
        totals_ps = core.ps(ctx, "totals_ps", [P, 512])
        lin_ps = core.ps(ctx, "lin_ps", [P, 512])
        att_ps = core.ps(ctx, "att_ps", [P, 512])
        fold_ps = core.ps(ctx, "fold_ps", [P, 512])
        bias_ps = core.ps(ctx, "bias_ps", [P, 512])
        bcast_ps = core.ps(ctx, "bcast_ps", [P, 512])
        e = core.edges
        block = ctx.enter_context(nc.Block())

        @block.sync
        def _(sp):
            sp.dma_start(e.src, io["src"]).then_inc(src_loaded, 16)
            sp.dma_start(e.dst, io["dst"]).then_inc(edges_loaded, 16)
            sp.dma_start(e.weight, io["edge_weight"]).then_inc(edges_loaded, 16)
            sp.wait_ge(cleared, 3)
            sp.dma_start(core.sorted.rearrange("(p c) r -> p c r", p=P), core.recs[:, :, :]).then_inc(sorted_cleared, 16)
            loads = w.layer0_loads(io)
            for dst, src in loads:
                sp.dma_start(dst, src, allow_slow_non_contiguous=True).then_inc(weights_loaded, 16)
            sp.wait_ge(weights_loaded, 16 * len(loads))
            sp.wait_ge(edges_loaded, 32)
            sp.wait_ge(sorted_cleared, 16)

        @block.gpsimd
        def _(pool):
            nc.gpsimd.iota(iota_i[:, :], [[1, P]], base=0, channel_multiplier=0).then_inc(consts_ready, 1)
            for t in (core.ident_f, core.ident_b, w.spread):
                nc.gpsimd.memset(t[:], 0.0).then_inc(masks, 1)
            for t in (core.before, core.not_before, core.ones_f):
                nc.gpsimd.memset(t[:], 1.0).then_inc(masks, 1)
            pool.wait_ge(masks, 6)
            for t in (core.ident_f, core.ident_b):
                nc.gpsimd.affine_select(out=t[:, :], in_=t[:, :], compare_op=ALU.not_equal, fill=1.0, base=0,
                                        pattern=[[-1, P]], channel_multiplier=1).then_inc(consts_ready, 1)
            nc.gpsimd.affine_select(out=core.before[:, :], in_=core.before[:, :], compare_op=ALU.is_gt, fill=0.0,
                                    base=0, pattern=[[1, P]], channel_multiplier=-1).then_inc(consts_ready, 1)
            nc.gpsimd.affine_select(out=core.not_before[:, :], in_=core.not_before[:, :], compare_op=ALU.is_ge,
                                    fill=0.0, base=0, pattern=[[-1, P]], channel_multiplier=1).then_inc(consts_ready, 1)
            sp_v = w.spread[:, :, :].rearrange("e a (b m) -> e a b m", b=2)
            nc.gpsimd.affine_select(out=sp_v, in_=sp_v, compare_op=ALU.not_equal, fill=1.0, base=0,
                                    pattern=[[-2, 2], [-1, 2], [0, 64]], channel_multiplier=1).then_inc(consts_ready, 1)
            nc.gpsimd.memset(core.zero_b[:, :], 0.0).then_inc(consts_ready, 1)
            nc.gpsimd.memset(core.s_src[:, :, :], 0.0).then_inc(consts_ready, 1)
            nc.gpsimd.memset(core.recs[:, :, 0:1], -1.0).then_inc(cleared, 1)
            nc.gpsimd.memset(core.recs[:, :, 1:2], 0.0).then_inc(cleared, 1)
            nc.gpsimd.memset(core.recs[:, :, 2:3], 0.0).then_inc(cleared, 1)
            pool.wait_ge(consts_ready, 8)
            pool.wait_ge(cleared, 3)

        @block.vector
        def _(dve):
            ch = Chain(dve, dve_own)
            dve.wait_ge(consts_ready, 1)
            ch.step(dve.tensor_copy(core.iota_f[:, :], iota_i[:, :]))
            ch.step(dve.memset(zeros[:, :], 0.0))
            dve.wait_ge(src_loaded, 16)
            ch.step(dve.tensor_scalar(e.tmp, e.src, 7, None, ALU.logical_shift_right))
            ch.link(dve.tensor_scalar(e.src, e.src, P - 1, None, ALU.bitwise_and))
            ch.step(dve.tensor_copy(e.tile, e.tmp))
            ch.link(dve.tensor_copy(e.row, e.src))
            setup_steps = ch.n
            with dve.Fori(0, T + 1) as t:
                lp = Chain(dve, dve_own, setup_steps + t * 3)
                for g in range(2):
                    lp.step(dve.tensor_scalar(e.half(e.junk, g), e.half(e.tile, g), core.iota_f[:, bass.ds(t, 1)], None,
                                              ALU.is_equal, ALU.add, accum_out=count[:, g:g + 1]))
                lp.wait()
                lp.link(dve.tensor_copy(hist[:, :, bass.ds(t, 1)].rearrange("p g a -> p (g a)"), count[:, :]))
            dve.sem_inc(hist_ready, 1)
            ch.n += 3 * (T + 1)
            dve.wait_ge(totals_ready, 1)
            ch.link(dve.tensor_scalar(npairs[:, :], totals_ps[:, 0:T + 1], float(PAIR - 1), None, ALU.add))
            ch.link(dve.tensor_copy(npairs_i[:, :], npairs[:, :]))
            ch.link(dve.tensor_scalar(npairs_i[:, :], npairs_i[:, :], 8, None, ALU.logical_shift_right))
            ch.link(dve.tensor_scalar(npairs[:, :], npairs_i[:, :], float(MIN_PAIRS), None, ALU.max))
            ch.step(dve.memset(first_pair[:, 0:1], 0.0))
            ch.link(dve.tensor_tensor_scan(first_pair[:, 1:T + 1], npairs[:, 0:T], zeros[:, 0:T], 0.0, ALU.add, ALU.add))
            ch.step(dve.tensor_scalar(core.base_f[:, :], first_pair[:, :], float(PAIR), None, ALU.mult))
            ch.step(dve.tensor_copy(core.pair_i[:, :], first_pair[:, :]))
            ch.link(dve.tensor_scalar(npairs[:, 0:1], first_pair[:, T:T + 1], float(RING), None, ALU.add))
            ch.link(dve.tensor_copy(core.rounds_i[:, :], npairs[:, 0:1]))
            ch.link(dve.tensor_scalar(core.rounds_i[:, :], core.rounds_i[:, :], 3, None, ALU.logical_shift_right))
            ch.link(dve.tensor_scalar(core.base_f[:, T:T + 1], core.base_f[:, T:T + 1], float(LOOK * PAIR), None, ALU.add))
            ch.link(dve.tensor_tensor(core.base2_f[:, :], core.base_f[:, :], bcast_ps[:, 0:T + 1], ALU.add))

        @block.tensor
        def _(pe):
            pe.wait_ge(consts_ready, 8)
            pe.wait_ge(lin_loaded, 96)
            for kb in range(2):
                for ib in range(2):
                    nc.tensor.transpose(lin_ps[:, kb * D + ib * P:kb * D + (ib + 1) * P], lin[:, ib, kb * P:(kb + 1) * P],
                                        core.ident_f[:, :])
            for b in range(4):
                last = nc.tensor.transpose(att_ps[:, b * HEADS:(b + 1) * HEADS], att[:, b * P:(b + 1) * P],
                                           core.ident_f[0:HEADS, 0:HEADS])
            last.then_inc(lin_t_psum, 1)
            pe.wait_ge(lin_t_ready, 2)
            for ib in range(2):
                for n, side in enumerate((1, 0)):
                    o = (ib * 2 + n) * HEADS
                    for kb in range(2):
                        nc.tensor.matmul(fold_ps[:, o:o + HEADS], lin_t[:, kb, ib * P:(ib + 1) * P],
                                         att_t[:, 2 * side + kb, :], start=(kb == 0), stop=(kb == 1))
            for n, side in enumerate((1, 0)):
                for kb in range(2):
                    last = nc.tensor.matmul(bias_ps[0:1, n * HEADS:(n + 1) * HEADS], b_lin[:, kb:kb + 1],
                                            att_t[:, 2 * side + kb, :], start=(kb == 0), stop=(kb == 1 and side == 0))
                if side == 1:
                    nc.tensor.matmul(bias_ps[0:1, 0:HEADS], core.ones_f[0:1, 0:1], b_parts[:, HD:ROW0],
                                     start=False, stop=True)
            last.then_inc(small_psum, 1)
            pe.wait_ge(bias_row_ready, 2)
            nc.tensor.matmul(bcast_ps[:, 0:ROW0 + HEADS], core.ones_f[0:1, :], bias_row[:, :],
                             start=True, stop=True).then_inc(bias_psum, 1)
            pe.wait_ge(hist_ready, 1)
            pe.wait_ge(small_ready, 1)
            nc.tensor.matmul(totals_ps[:, 0:T + 1], core.ones_f[:, :], hist[:, 0, :], start=True, stop=False)
            nc.tensor.matmul(totals_ps[:, 0:T + 1], core.ones_f[:, :], hist[:, 1, :], start=False, stop=True)
            nc.tensor.matmul(bcast_ps[:, 0:T + 1], core.ones_f[:, :], hist[:, 0, :], start=True, stop=True)\
                .then_inc(totals_ready, 1)

        @block.scalar
        def _(act):
            act.dma_start(lin[:, :, :], io["L0_gnn_W_lin"].rearrange("(b p) n -> p b n", p=P)).then_inc(lin_loaded, 16)
            act.dma_start(att[:, :], io["L0_gnn_att_w"]).then_inc(lin_loaded, 16)
            act.dma_start(b_lin[:, :], io["L0_gnn_b_lin"].rearrange("(b p) -> p b", p=P),
                          allow_slow_non_contiguous=True).then_inc(lin_loaded, 16)
            act.dma_start(b_parts[:, 0:HD], io["L0_gnn_emb_b"].rearrange("(a n) -> a n", a=1)).then_inc(lin_loaded, 16)
            act.dma_start(b_parts[:, HD:ROW0], io["L0_gnn_att_b"].rearrange("(a n) -> a n", a=1)).then_inc(lin_loaded, 16)
            act.dma_start(w.small[:, :, 0:HD], io["L0_gnn_emb_w"].rearrange("(b p) n -> p b n", p=P)).then_inc(lin_loaded, 16)
            act.wait_ge(lin_t_psum, 1)
            nc.scalar.activation(flat(lin_t[:, :, :]), lin_ps[:, :], ACT.Copy).then_inc(lin_t_ready, 1)
            nc.scalar.activation(flat(att_t[:, :, :]), att_ps[:, 0:4 * HEADS], ACT.Copy).then_inc(lin_t_ready, 1)
            act.wait_ge(lin_loaded, 96)
            act.wait_ge(small_psum, 1)
            nc.scalar.activation(w.small[:, :, HD:HD + 2 * HEADS], fold_ps[:, 0:4 * HEADS].rearrange("p (b n) -> p b n", b=2),
                                 ACT.Copy).then_inc(act_own, 1)
            nc.scalar.activation(bias_row[:, 0:HD], b_parts[:, 0:HD], ACT.Copy).then_inc(bias_row_ready, 1)
            nc.scalar.activation(bias_row[:, HD:ROW0 + HEADS], bias_ps[0:1, 0:2 * HEADS], ACT.Copy)\
                .then_inc(bias_row_ready, 1)
            act.wait_ge(bias_psum, 1)
            nc.scalar.activation(w.small_bias[:, :], bcast_ps[:, 0:ROW0 + HEADS], ACT.Copy).then_inc(act_own, 1)
            act.wait_ge(act_own, 2)
            act.sem_inc(small_ready, 1)


def bucket(core, w):
    nc, io = core.nc, core.io
    with ExitStack() as ctx:
        sem = lambda n: core.sem(ctx, n)
        onehot_ready, ranks_psum, rank_read = sem("onehot_ready"), sem("ranks_psum"), sem("rank_read")
        slots_ready, recs_ready = sem("slots_ready"), sem("recs_ready")
        scattered = [sem(f"scattered{h}") for h in range(2)]
        x_loaded, xn_ready, xnt_psum, xnt_ready = sem("x_loaded"), sem("xn_ready"), sem("xnt_psum"), sem("xnt_ready")
        table_psum, table_ready, table_stored = sem("table_psum"), sem("table_ready"), sem("table_stored")
        col_own, node_own, act_own = sem("col_own"), sem("node_own"), sem("act_own")
        rest_psum, sorted_loaded, halves = sem("rest_psum"), sem("sorted_loaded"), sem("halves")

        onehot = core.sb("onehot", [P, 4, T + 1], BF16, ctx)
        rank_junk = core.sb("rank_junk", [P, 4, T + 1], ctx=ctx)
        slot_f = core.sb("slot_f", [P, 2, HALF], ctx=ctx)
        slot_i = core.sb("slot_i", [P, 2, HALF], I32, ctx)
        slot_p = core.sb("slot_p", [P, 2, HALF], I32, ctx)
        slot_at = core.sb("slot_at", [P, SLOTS], U32, ctx)
        rec = core.sb("rec", [P, SLOTS, REC], ctx=ctx)
        x = core.sb("x_node", [P, 2, D], ctx=ctx)
        xn = core.sb("xn_node", [P, D], ctx=ctx)
        xnt = core.sb("xnt_node", [P, 2, P], ctx=ctx)
        stats = core.sb("stats", [P, 6], ctx=ctx)
        mv = core.sb("mv", [P, 2], ctx=ctx)
        rstd = core.sb("rstd", [P, 1], ctx=ctx)
        tmp = core.sb("rstd_tmp", [P, 1], ctx=ctx)
        row = core.sb("row", [P, 2, ROW0 + HEADS], ctx=ctx)
        rest = core.sb("rest", [P, HEADS], ctx=ctx)
        counts_ps = core.ps(ctx, "counts_ps", [P, 2, 512])
        xnt_ps = core.ps(ctx, "xnt_ps", [P, 512])
        table_ps = core.ps(ctx, "table_ps", [P, 512])
        e = core.edges
        x_v = io["x"].rearrange("(t p) d -> t p d", p=P)
        tab_v = core.tab0.rearrange("(t p) d -> t p d", p=P)
        block = ctx.enter_context(nc.Block())
        COL_STEPS = 2 * 3
        NORM_STEPS = 3 + 12 + 1
        NODE_STEPS = NORM_STEPS + 5

        @block.sync
        def _(sp):
            def load(k):
                sp.dma_start(x[:, bass.ds(k % 2, 1), :], x_v[bass.ds(k, 1), :, :].rearrange("t p d -> p t d"))\
                    .then_inc(x_loaded, 16)

            def store(k):
                sp.wait_ge(table_ready, k + 1)
                sp.dma_start(tab_v[bass.ds(k, 1), :, :].rearrange("t p d -> p t d"),
                             row[:, bass.ds(k % 2, 1), 0:ROW0]).then_inc(table_stored, 16)

            load(0)
            with sp.Fori(0, TR - 1) as k:
                sp.wait_ge(xn_ready, k + AHEAD)
                sp.wait_ge(x_loaded, k * 16 + 16)
                load(k + 1)
                store(k)
                sp.wait_ge(table_ready, 1)
                sp.wait_ge(table_stored, k * 16 + 16)
            store(TR - 1)
            sp.wait_ge(table_stored, TR * 16)
            for h in range(2):
                sp.wait_ge(scattered[h], 16 * HALF * (EJ // SLOTS))
            sp.dma_start(core.recs[:, :, :], core.sorted.rearrange("(p c) r -> p c r", p=P)).then_inc(sorted_loaded, 16)
            sp.wait_ge(sorted_loaded, 16)

        @block.gpsimd
        def _(pool):
            with pool.Fori(0, EJ // SLOTS) as k:
                for h in range(2):
                    pool.wait_ge(recs_ready, 2 * k + (h + 1))
                    pool.wait_ge(slots_ready, 2 * k + (h + 1))
                    pool.sem_inc(halves, 1)
                    for s in range(h * HALF, (h + 1) * HALF):
                        nc.gpsimd.indirect_dma_start(core.sorted, bass.IndirectOffsetOnAxis(ap=slot_at[:, s:s + 1], axis=0),
                                                     rec[:, s, :], None).then_inc(scattered[h], 16)

        @block.vector
        def _(dve):
            dve.sem_inc(xn_ready, AHEAD)

            def columns(k, h, first):
                ch = Chain(dve, col_own, k * COL_STEPS + h * (COL_STEPS // 2))
                j0 = k * SLOTS + h * HALF

                def bucket_onehot(c):
                    dve.wait_ge(rest_psum, j0 + (c - 3 + AHEAD))
                    dve.tensor_scalar(onehot[:, c % 4, :], core.iota_f[:, 0:T + 1],
                                      e.half(e.tile, c % 2)[:, bass.ds(k * HALF + (h * HALF + c) // 2, 1)], None,
                                      ALU.is_equal).then_inc(onehot_ready, 1)

                for c in range(3):
                    bucket_onehot(c)
                for c in range(HALF):
                    if c + 3 < HALF:
                        bucket_onehot(c + 3)
                    dve.wait_ge(ranks_psum, j0 + (c + 1))
                    if c == 0:
                        dve.wait_ge(onehot_ready, j0 + 1)
                    if c == 0 and not first:
                        ch.wait()
                    dve.tensor_tensor_reduce(out=rank_junk[:, c % 4, :], in0=counts_ps[:, c % 2, 0:T + 1],
                                             in1=onehot[:, c % 4, :], scale=1.0, scalar=0.0, op0=ALU.mult, op1=ALU.add,
                                             accum_out=slot_f[:, h, c:c + 1]).then_inc(rank_read, 1)
                dve.wait_ge(rank_read, k * SLOTS + (h + 1) * HALF)
                ch.link(dve.tensor_copy(slot_i[:, h, :], slot_f[:, h, :]))
                ch.step(dve.tensor_scalar(slot_p[:, h, :], slot_i[:, h, :], P - 1, None, ALU.bitwise_and))
                ch.link(dve.tensor_scalar(slot_i[:, h, :], slot_i[:, h, :], 7, None, ALU.logical_shift_right))
                if not first:
                    dve.wait_ge(scattered[h], k * (16 * HALF))
                dve.scalar_tensor_tensor(slot_at[:, h * HALF:(h + 1) * HALF], slot_p[:, h, :], float(CS), slot_i[:, h, :],
                                         ALU.mult, ALU.add).then_inc(slots_ready, 1)

            def node_norm(k, first):
                ch = Chain(dve, node_own, k * NODE_STEPS)
                dve.wait_ge(x_loaded, 16 * k + 16)
                xk = x[:, bass.ds(k % 2, 1), :]
                if not first:
                    ch.wait()
                ch.step(dve.bn_stats(stats[:, :], xk))
                ch.wait_apart()
                ch.link(dve.bn_aggr(mv[:, :], stats[:, :]))
                rstd_steps(dve, ch, mv[:, 1:2], rstd[:, :], tmp[:, :])
                dve.wait_ge(xnt_psum, k + AHEAD)
                ch.step(dve.tensor_scalar(xn[:, :].unsqueeze(1), xk, mv[:, 0:1], rstd[:, :], ALU.subtract, ALU.mult))
                ch.wait()
                dve.sem_inc(xn_ready, 1)
                assert ch.n == NORM_STEPS, ch.n

            def node_row(k, first):
                ch = Chain(dve, node_own, k * NODE_STEPS + NORM_STEPS)
                dve.wait_ge(table_psum, k + 1)
                if not first:
                    dve.wait_ge(table_stored, k * 16)
                rk = row[:, bass.ds(k % 2, 1), :]
                ch.link(dve.tensor_tensor(rk, table_ps[:, 0:ROW0 + HEADS].unsqueeze(1), w.small_bias[:, :].unsqueeze(1),
                                          ALU.add))
                dve.sem_inc(table_ready, 1)
                rs, re = rk[:, :, ROW0:ROW0 + HEADS], rest[:, :].unsqueeze(1)
                part = lambda n: core.s_src[:, bass.ds(k, 1), n * HEADS:(n + 1) * HEADS]
                ch.link(dve.tensor_copy(part(0), rs))
                ch.link(dve.tensor_tensor(re, rs, part(0), ALU.subtract))
                ch.link(dve.tensor_copy(part(1), re))
                ch.link(dve.tensor_tensor(part(2), re, part(1), ALU.subtract))
                assert NORM_STEPS + ch.n == NODE_STEPS, ch.n

            def iteration(k, first):
                columns(k, 0, first)
                node_norm(k, first)
                columns(k, 1, first)
                node_row(k, first)

            iteration(0, True)
            with dve.Fori(1, TR) as k:
                iteration(k, False)

        @block.tensor
        def _(pe):
            nc.tensor.matmul(counts_ps[:, 0, 0:T + 1], core.ones_f[0:1, :], core.base_f[0:1, :], start=True, stop=True)
            nc.tensor.matmul(counts_ps[:, 1, 0:T + 1], core.ones_f[0:1, :], core.base2_f[0:1, :], start=True, stop=True)
            pe.sem_inc(rest_psum, AHEAD)
            pe.sem_inc(xnt_psum, AHEAD)

            def columns(k, h):
                j0 = k * SLOTS + h * HALF

                def rest(c):
                    pe.wait_ge(rank_read, j0 + (c + 1))
                    nc.tensor.matmul(counts_ps[:, c % 2, 0:T + 1], core.not_before[:, :], onehot[:, c % 4, :], start=False,
                                     stop=True, skip_group_check=True).then_inc(rest_psum, 1)

                for c in range(HALF):
                    if c >= 2:
                        rest(c - 2)
                    pe.wait_ge(onehot_ready, j0 + (c + 1))
                    nc.tensor.matmul(counts_ps[:, c % 2, 0:T + 1], core.before[:, :], onehot[:, c % 4, :], start=False,
                                     stop=True, skip_group_check=True).then_inc(ranks_psum, 1)
                rest(HALF - 2)
                rest(HALF - 1)

            with pe.Fori(0, TR) as k:
                columns(k, 0)
                pe.wait_ge(xn_ready, k + 1 + AHEAD)
                for b in range(2):
                    last = nc.tensor.transpose(xnt_ps[:, b * P:(b + 1) * P], xn[:, b * P:(b + 1) * P], core.ident_f[:, :])
                last.then_inc(xnt_psum, 1)
                pe.wait_ge(xnt_ready, k + 1)
                for b in range(2):
                    last = nc.tensor.matmul(table_ps[:, 0:ROW0 + HEADS], xnt[:, b, :], w.small[:, b, :],
                                            start=(b == 0), stop=(b == 1))
                last.then_inc(table_psum, 1)
                columns(k, 1)

        @block.scalar
        def _(act):
            def iteration(k, first):
                for h in range(2):
                    j0 = k * HALF + h * (HALF // 2)
                    if not first:
                        act.wait_ge(scattered[h], k * (16 * HALF))
                    for n, src in enumerate((e.row, e.weight, e.dst)):
                        out = rec[:, h * HALF:(h + 1) * HALF, n].rearrange("p (j g) -> p g j", g=2)
                        out = out.bitcast(I32) if n == 2 else out
                        last = nc.scalar.activation(out, src.rearrange("p (g j) -> p g j", g=2)[:, :, bass.ds(j0, HALF // 2)],
                                                    ACT.Copy)
                        last.then_inc(act_own, 1)
                    act.wait_ge(act_own, (2 * k + h + 1) * 3)
                    act.sem_inc(recs_ready, 1)
                    if h == 0:
                        act.wait_ge(xnt_psum, k + 1 + AHEAD)
                        nc.scalar.activation(flat(xnt[:, :, :]), xnt_ps[:, 0:2 * P], ACT.Copy).then_inc(xnt_ready, 1)

            iteration(0, True)
            with act.Fori(1, TR) as k:
                iteration(k, False)
            act.wait_ge(act_own, 6 * TR)


def gather_rounds(core, pool, idx_ready, used, used_count, gathered, table, width, idx, ring):
    rounds = pool.snap(pool.value_load(core.rounds_i[0:1, 0:1], min_val=1, max_val=CS // SLOTS + 1))
    with pool.Fori(0, rounds) as r:
        for k in range(RING):
            pool.wait_ge(used, used_count(r * RING + k))
            pool.wait_ge(idx_ready, r * RING + (k + 1))
            pool.sem_inc(core.rounds, 1)
            for c in range(2):
                core.nc.gpsimd.indirect_dma_start(ring[:, 2 * k + c, 0:width], None, table,
                                                  bass.IndirectOffsetOnAxis(ap=idx[:, 2 * k + c:2 * k + c + 1], axis=0))\
                    .then_inc(gathered[k], 16)


def relay_rounds(core, sp, gathered, landed):
    rounds = sp.snap(sp.value_load(core.rounds_i[0:1, 0:1], min_val=1, max_val=CS // SLOTS + 1))
    with sp.Fori(0, rounds) as r:
        for k in range(RING):
            sp.wait_ge(gathered[k], r * 32 + FAR)
            sp.sem_inc(landed, 1)


def tile_pairs(core, eng, t):
    lo = eng.snap(eng.value_load(core.pair_i[0:1, bass.ds(t, 1)], min_val=0, max_val=MAX_PAIRS))
    hi = eng.snap(eng.value_load(core.pair_i[0:1, bass.ds(t + 1, 1)], min_val=MIN_PAIRS, max_val=MAX_PAIRS))
    return lo, hi


def idle(*_):
    pass


def over_tiles(core, eng, pair, tile_end, stages):
    def supertile(s, first):
        for i in range(QUAD):
            t = s * QUAD + i
            lo, hi = tile_pairs(core, eng, t)
            pair(lo, t, i, True, False)
            if not (first and i == 0):
                tile_end(t - 1, (i - 1) % QUAD, s if i else s - 1, lo)
            if not first:
                stages[2 * i](s - 1)
            with eng.Fori(lo + 1, hi - 1) as q:
                pair(q, t, i, False, False)
            pair(hi - 1, t, i, False, True)
            if not first:
                stages[2 * i + 1](s - 1)

    supertile(0, True)
    supertile(1, False)
    with eng.Fori(2, ST) as s:
        supertile(s, False)
    last = eng.snap(eng.value_load(core.pair_i[0:1, T:T + 1], min_val=0, max_val=MAX_PAIRS))
    tile_end(T - 1, QUAD - 1, ST - 1, last)
    for stage in stages:
        stage(ST - 1)


def layer0(core, w):
    nc, io = core.nc, core.io
    with ExitStack() as ctx:
        sem = lambda n: core.sem(ctx, n)
        core.rounds = sem("rounds")
        gathered = [sem(f"gathered{k}") for k in range(RING)]
        idx_ready, landed = sem("idx_ready"), sem("landed")
        onehot_ready, turned_psum, turned_ready = sem("onehot_ready"), sem("turned_psum"), sem("turned_ready")
        score_psum, z_ready, weight_ready = sem("score_psum"), sem("z_ready"), sem("weight_ready")
        msg_ready, onehot_f_ready, agg_done, agg_free = sem("msg_ready"), sem("onehot_f_ready"), sem("agg_done"), sem("agg_free")
        tanh_own, dve_tile, dve_dense = sem("tanh_own"), sem("dve_tile"), sem("dve_dense")
        x_loaded, xn_ready, pe_job, act_job, dve_job = sem("x_loaded"), sem("xn_ready"), sem("pe_job"), sem("act_job"), sem("dve_job")
        gate_ready, dense_done, stored = sem("gate_ready"), sem("dense_done"), sem("stored")

        idx = core.sb("idx", [P, SLOTS], U32, ctx)
        ring = core.sb("ring0", [P, SLOTS, ROW0], ctx=ctx)
        onehot = core.sb("onehot0", [P, 4, 2 * P], BF16, ctx)
        onehot_f = core.sb("onehot_f", [P, 2, P], ctx=ctx)
        turned = core.sb("turned", [P, 2, 2 * P], BF16, ctx)
        z = core.sb("z", [P, 2, 2 * HEADS], ctx=ctx)
        th = core.sb("th", [P, 2, 2 * HEADS], ctx=ctx)
        msg = core.sb("msg", [P, 2, 2, MSG0], ctx=ctx)
        half = core.sb("half", [P, 1], ctx=ctx)
        xb = core.sb("xb", [P, 2, QUAD, D], ctx=ctx)
        den = core.sb("den", [P, HEADS], ctx=ctx)
        den0 = core.sb("den0", [P, HEADS], ctx=ctx)
        stats = core.sb("stats0", [P, QUAD, 6], ctx=ctx)
        mv = core.sb("mv0", [P, QUAD, 2], ctx=ctx)
        mv2 = core.sb("mv20", [P, QUAD, 2], ctx=ctx)
        stats2 = core.sb("stats20", [P, QUAD, 6], ctx=ctx)
        var = core.sb("var0", [P, QUAD], ctx=ctx)
        rstd = core.sb("rstd0", [P, QUAD], ctx=ctx)
        rtmp = core.sb("rtmp0", [P, QUAD], ctx=ctx)
        xn = core.sb("xn0", [P, QUAD, D], ctx=ctx)
        xn2 = core.sb("xn20", [P, QUAD, D], ctx=ctx)
        xt = core.sb("xt0", [P, 2, TOK], ctx=ctx)
        h1 = core.sb("h1", [P, 2 + EXPERTS, TOK], ctx=ctx)
        h2 = core.sb("h2", [P, 3, TOK], ctx=ctx)
        gate = core.sb("gate", [P, 6, QUAD, EXPERTS], ctx=ctx)
        gsum = core.sb("gsum", [P, 3, QUAD], ctx=ctx)
        coef = core.sb("coef", [P, QUAD, EXPERTS + 1], ctx=ctx)
        coef_t = core.sb("coef_t", [EXPERTS + 1, TOK], ctx=ctx)
        pair_ps = core.ps(ctx, "pair_ps", [P, 2, 512])
        turned_ps = pair_ps[:, :, 0:P].bitcast(BF16)
        score_ps = pair_ps[:, :, 2 * P:2 * P + 2 * HEADS]
        agg_ps = core.ps(ctx, "agg_ps", [P, 2, 512])
        bank = [core.ps(ctx, f"bank{b}", [P, 512]) for b in range(4)]
        block = ctx.enter_context(nc.Block())
        x_v = io["x"].rearrange("(s i p) d -> s p i d", i=QUAD, p=P)
        tab1_v = core.tab1.rearrange("(s i p) d -> s p i d", i=QUAD, p=P)
        NJ, NA, ND = 17, 14, 5

        @block.sync
        def _(sp):
            relay_rounds(core, sp, gathered, landed)

        @block.gpsimd
        def _(pool):
            gather_rounds(core, pool, idx_ready, msg_ready, lambda q: q + (1 - RING + AHEAD), gathered, core.tab0, ROW0, idx, ring)

        @block.vector
        def _(dve):
            TILE = 3 + 4 + 3
            dve.sem_inc(msg_ready, AHEAD)
            dve.sem_inc(z_ready, AHEAD)
            dve.sem_inc(dve_job, AHEAD)
            dve.sem_inc(agg_free, AHEAD)
            dve.sem_inc(dense_done, AHEAD)
            dve.memset(coef[:, :, :], 1.0).then_inc(gate_ready, AHEAD)
            dve.memset(half[:, :], 0.5).then_inc(xn_ready, AHEAD)

            def indices(q):
                dve.tensor_copy(idx[:, bass.ds((q % RING) * 2, 2)], core.recs[:, bass.ds(q * 2, 2), 2].bitcast(I32))\
                    .then_inc(idx_ready, 1)

            def onehots(q, first=False):
                if not first:
                    dve.wait_ge(onehot_f_ready, 2 * q - 6 + AHEAD)
                for c in range(2):
                    dve.tensor_scalar(onehot[:, bass.ds(q % 4, 1), c * P:(c + 1) * P], core.iota_f[:, :].unsqueeze(1),
                                      core.recs[:, bass.ds(q * 2 + c, 1), 0], None, ALU.is_equal).then_inc(onehot_ready, 1)

            def scores(q):
                dve.wait_ge(landed, q + 1)
                dve.wait_ge(score_psum, q + 1 + AHEAD)
                dve.wait_ge(weight_ready, q - 1 + AHEAD)
                dve.tensor_tensor(z[:, bass.ds(q % 2, 1), :].rearrange("p a (c h) -> p (a c) h", c=2),
                                  score_ps[:, bass.ds(q % 2, 1), :].rearrange("p a (c h) -> p (a c) h", c=2),
                                  ring[:, bass.ds((q % RING) * 2, 2), HD:ROW0], ALU.add).then_inc(z_ready, 1)

            def pair(q, t, i, first_of_tile, last_of_tile):
                onehots(q + 2)
                dve.wait_ge(weight_ready, q + 1 + AHEAD)
                dve.wait_ge(agg_done, 2 * q - 2 + AHEAD)
                for c in range(2):
                    m = msg[:, bass.ds(q % 2, 1), c, :].rearrange("p a m -> p (a m)")
                    last = dve.tensor_tensor(m[:, 0:HEADS * HD].rearrange("p (h d) -> p h d", h=HEADS),
                                             ring[:, bass.ds((q % RING) * 2 + c, 1), 0:HD].broadcast_to([P, HEADS, HD]),
                                             m[:, HEADS * HD:MSG0].unsqueeze(2).broadcast_to([P, HEADS, HD]), ALU.mult)
                last.then_inc(msg_ready, 1)
                indices(q + RING)
                scores(q + 1)

            def tile_end(t, i, s, q_end):
                ch = Chain(dve, dve_tile, t * TILE)
                a = agg_ps[:, i % 2, :]
                dve.wait_ge(agg_done, 2 * q_end + AHEAD)
                if i == 0:
                    dve.wait_ge(x_loaded, s * 16 + 16)
                if not (isinstance(t, int) and t == 0):
                    ch.wait()
                ch.link(dve.tensor_scalar(den0[:, :], a[:, HEADS * HD:MSG0], 0.0, None, ALU.is_equal))
                ch.link(dve.tensor_tensor(den[:, :], den0[:, :], a[:, HEADS * HD:MSG0], ALU.add))
                ch.link(dve.reciprocal(den[:, :], den[:, :]))
                xt_ = xb[:, bass.ds(s % 2, 1), i, :]
                for h in range(HEADS):
                    o = xt_[:, :, h * HD:(h + 1) * HD]
                    ch.step(dve.scalar_tensor_tensor(o, a[:, h * HD:(h + 1) * HD].unsqueeze(1), den[:, h:h + 1], o,
                                                     ALU.mult, ALU.add))
                ch.wait()
                dve.sem_inc(agg_free, 1)
                ch.step(dve.bn_stats(stats[:, i, :], xt_))
                ch.wait_apart()
                ch.step(dve.bn_aggr(mv[:, i, :], stats[:, i, :]))
                assert ch.n == TILE

            for q in range(RING):
                indices(q)
            onehots(0, True)
            onehots(1, True)
            scores(0)

            def normalize(ch, mvs, src, out):
                ch.link(dve.tensor_copy(var[:, :], mvs[:, :, 1]))
                rstd_steps(dve, ch, var[:, :], rstd[:, :], rtmp[:, :])
                for i in range(QUAD):
                    ch.step(dve.tensor_scalar(out[:, i, :].unsqueeze(1), src[:, :, i, :], mvs[:, i, 0:1], rstd[:, i:i + 1],
                                              ALU.subtract, ALU.mult))
                ch.wait()

            NORM = 1 + 12 + 4
            S0, S1, S2, S3 = NORM, 3 + 6 + 12 + 5, 2, 2 + 9 + NORM + 1
            S = S0 + S1 + S2 + S3

            def stage0(s):
                ch = Chain(dve, dve_dense, s * S)
                dve.wait_ge(pe_job, NJ * s - NJ + 2 + FAR)
                dve.wait_ge(dve_tile, (s * QUAD + QUAD) * TILE)
                if not (isinstance(s, int) and s == 0):
                    ch.wait()
                normalize(ch, mv, xb[:, bass.ds(s % 2, 1), :, :], xn)
                dve.sem_inc(xn_ready, 1)
                assert ch.n == S0, ch.n

            def stage1(s):
                ch = Chain(dve, dve_dense, s * S + S0)
                g = lambda n: gate[:, n, :, :]
                dve.wait_ge(pe_job, NJ * s + 3 + FAR)
                lg = bank[2][:, 0:QUAD * EXPERTS].rearrange("p (i e) -> p i e", i=QUAD)
                ch.link(dve.tensor_tensor(g(0), lg, w.gate_bias[:, :].unsqueeze(1).broadcast_to([P, QUAD, EXPERTS]), ALU.add))
                dve.sem_inc(dve_job, 1)
                b4 = lambda v: v.unsqueeze(2).broadcast_to([P, QUAD, EXPERTS])
                ch.link(dve.tensor_reduce(gsum[:, 0, :], g(0), mybir.AxisListType.X, ALU.max))
                ch.link(dve.tensor_tensor(g(1), g(0), b4(gsum[:, 0, :]), ALU.subtract))
                dve.sem_inc(gate_ready, 1)
                dve.wait_ge(act_job, s * NA + 5 + AHEAD)
                ch.link(dve.tensor_reduce(gsum[:, 1, :], g(2), mybir.AxisListType.X, ALU.add))
                ch.link(dve.reciprocal(gsum[:, 2, :], gsum[:, 1, :]))
                ch.link(dve.tensor_tensor(g(0), g(2), b4(gsum[:, 2, :]), ALU.mult))
                ch.link(dve.tensor_reduce(gsum[:, 0, :], g(0), mybir.AxisListType.X, ALU.max))
                ch.link(dve.tensor_tensor(g(1), g(0), b4(gsum[:, 0, :]), ALU.subtract))
                ch.link(dve.memset(g(3), 0.0))
                dve.sem_inc(gate_ready, 1)
                for d in range(1, EXPERTS):
                    lo, hi = g(0)[:, :, 0:EXPERTS - d], g(0)[:, :, d:EXPERTS]
                    ch.link(dve.tensor_tensor(g(4)[:, :, 0:EXPERTS - d], lo, hi, ALU.is_ge))
                    ch.link(dve.tensor_tensor(g(3)[:, :, 0:EXPERTS - d], g(3)[:, :, 0:EXPERTS - d],
                                              g(4)[:, :, 0:EXPERTS - d], ALU.add))
                    ch.link(dve.tensor_tensor(g(4)[:, :, 0:EXPERTS - d], lo, hi, ALU.is_lt))
                    ch.link(dve.tensor_tensor(g(3)[:, :, d:EXPERTS], g(3)[:, :, d:EXPERTS],
                                              g(4)[:, :, 0:EXPERTS - d], ALU.add))
                ch.link(dve.tensor_scalar(g(3), g(3), 2.0, None, ALU.is_ge))
                dve.wait_ge(act_job, s * NA + 8 + AHEAD)
                ch.link(dve.tensor_tensor(g(1), g(2), g(3), ALU.mult))
                ch.link(dve.tensor_reduce(gsum[:, 1, :], g(1), mybir.AxisListType.X, ALU.add))
                ch.link(dve.reciprocal(gsum[:, 2, :], gsum[:, 1, :]))
                ch.link(dve.tensor_tensor(coef[:, :, 0:EXPERTS], g(1), b4(gsum[:, 2, :]), ALU.mult))
                dve.sem_inc(gate_ready, 1)
                assert ch.n == S1, ch.n

            def stage2(s):
                ch = Chain(dve, dve_dense, s * S + S0 + S1)
                for n, (job, b) in enumerate(((13, 0), (15, 2))):
                    dve.wait_ge(act_job, s * NA + (13, 14)[n] + AHEAD)
                    dve.wait_ge(pe_job, NJ * s + job + FAR)
                    ch.link(dve.tensor_tensor(h2[:, 1 + n, :], h2[:, 1 + n, :], bank[b][:, :], ALU.mult))
                    dve.sem_inc(dve_job, 1)
                assert ch.n == S2

            def stage3(s):
                ch = Chain(dve, dve_dense, s * S + S0 + S1 + S2)
                x2 = xb[:, bass.ds(s % 2, 1), :, :]
                for n, b in enumerate((3, 0)):
                    dve.wait_ge(pe_job, NJ * s + 16 + n + FAR)
                    o = x2[:, :, 2 * n:2 * n + 2, :].rearrange("p a i d -> p (a i) d")
                    ch.link(dve.tensor_tensor(o, o, bank[b][:, :].rearrange("p (i d) -> p i d", i=2), ALU.add))
                    dve.sem_inc(dve_job, 1)
                for i in range(QUAD):
                    ch.step(dve.bn_stats(stats2[:, i, :], x2[:, :, i, :]))
                ch.wait_apart()
                for i in range(QUAD):
                    ch.step(dve.bn_aggr(mv2[:, i, :], stats2[:, i, :]))
                ch.wait()
                if not (isinstance(s, int) and s == 0):
                    dve.wait_ge(stored, s * 16)
                normalize(ch, mv2, x2, xn2)
                ch.link(dve.tensor_tensor(core.rows[:, bass.ds(s * QUAD, QUAD), :], xn2[:, :, :],
                                          x2.rearrange("p a i d -> p (a i) d"), ALU.add))
                dve.sem_inc(dense_done, 1)
                assert ch.n == S3, ch.n

            over_tiles(core, dve, pair, tile_end, (stage0, idle, stage1, idle, idle, stage2, idle, stage3))

        @block.tensor
        def _(pe):
            pe.sem_inc(score_psum, AHEAD)
            pe.sem_inc(agg_done, AHEAD)
            pe.sem_inc(pe_job, FAR)

            def turn(q):
                pe.wait_ge(onehot_ready, 2 * q + 2)
                pe.wait_ge(turned_ready, q - 1 + AHEAD)
                pe.wait_ge(z_ready, q - 1 + AHEAD)
                for c in range(2):
                    last = nc.tensor.transpose(turned_ps[:, bass.ds(q % 2, 1), c * P:(c + 1) * P],
                                               onehot[:, bass.ds(q % 4, 1), c * P:(c + 1) * P].rearrange("p a b -> p (a b)"),
                                               core.ident_b[:, :])
                last.then_inc(turned_psum, 1)

            def score(q, t):
                pe.wait_ge(turned_ready, q + 1 + AHEAD)
                for c in range(2):
                    for n in range(3):
                        last = nc.tensor.matmul(score_ps[:, bass.ds(q % 2, 1), c * HEADS:(c + 1) * HEADS].rearrange("p a h -> p (a h)"),
                                                turned[:, bass.ds(q % 2, 1), c * P:(c + 1) * P].rearrange("p a b -> p (a b)"),
                                                core.s_src[:, bass.ds(t, 1), n * HEADS:(n + 1) * HEADS].rearrange("p a b -> p (a b)"),
                                                start=(n == 0), stop=(n == 2), skip_group_check=True)
                last.then_inc(score_psum, 1)

            def pair(q, t, i, first_of_tile, last_of_tile):
                turn(q + 2)
                score(q + 1, t + 1 if last_of_tile else t)
                agg = agg_ps[:, i % 2, 0:MSG0]
                if first_of_tile:
                    pe.wait_ge(agg_free, t - 1 + AHEAD)
                    nc.tensor.matmul(agg, core.zero_b[:, 0:P], core.zero_b[:, P:P + MSG0], start=True, stop=False,
                                     skip_group_check=True)
                pe.wait_ge(msg_ready, q + 1 + AHEAD)
                for c in range(2):
                    pe.wait_ge(onehot_f_ready, 2 * q + (c + 1) + AHEAD)
                    nc.tensor.matmul(agg, onehot_f[:, c, :], msg[:, bass.ds(q % 2, 1), c, :].rearrange("p a m -> p (a m)"),
                                     start=False, stop=last_of_tile and c == 1, skip_group_check=True).then_inc(agg_done, 1)

            def linear(out, w_blocks, x_blocks):
                for n, (a, b) in enumerate(zip(w_blocks, x_blocks)):
                    last = nc.tensor.matmul(out, a, b, start=(n == 0), stop=(n == len(w_blocks) - 1))
                return last

            def job(s, n, act=None, dve=None):
                if act is not None:
                    pe.wait_ge(act_job, s * NA + (act + AHEAD))
                if dve is not None:
                    pe.wait_ge(dve_job, s * ND + (dve + AHEAD))

            def h1_block(s, n, b, act=None, dve=None):
                job(s, n, act, dve)
                linear(bank[b][:, :], [w.up1[:, k, (n - 4) * P:(n - 3) * P] for k in range(2)],
                       [xt[:, k, :] for k in range(2)]).then_inc(pe_job, 1)

            def stage0(s):
                pe.wait_ge(xn_ready, s + 1 + AHEAD)
                for b in range(2):
                    job(s, 1 + b, *((None, 0), (0, None))[b])
                    for i in range(QUAD):
                        last = nc.tensor.transpose(bank[b][:, i * P:(i + 1) * P], xn[:, i, b * P:(b + 1) * P], core.ident_f[:, :])
                    last.then_inc(pe_job, 1)
                job(s, 3, 2, -2)
                for i in range(QUAD):
                    last = linear(bank[2][:, i * EXPERTS:(i + 1) * EXPERTS], [xt[:, k, i * P:(i + 1) * P] for k in range(2)],
                                  [w.gate[:, k, :] for k in range(2)])
                last.then_inc(pe_job, 1)
                h1_block(s, 4, 3, None, -1)
                h1_block(s, 5, 0, 1)

            def stage1(s):
                h1_block(s, 6, 1, 2)
                h1_block(s, 7, 2, None, 1)
                h1_block(s, 8, 3, 3)
                h1_block(s, 9, 0, 4)

            def stage2(s):
                pe.wait_ge(gate_ready, s * 3 + 3 + AHEAD)
                job(s, 10, 6)
                for i in range(QUAD):
                    last = nc.tensor.transpose(bank[1][0:EXPERTS + 1, i * P:(i + 1) * P], coef[:, i, :], core.ident_f[:, :])
                last.then_inc(pe_job, 1)
                job(s, 11, 7)
                linear(bank[2][:, :], [w.up2[:, k, :] for k in range(2)], [h1[:, k, :] for k in range(2)]).then_inc(pe_job, 1)
                for n in range(2):
                    job(s, 12 + 2 * n, (10, 11)[n])
                    for m in range(2):
                        e = 2 * n + m
                        last = nc.tensor.matmul(bank[(3, 1)[n]][m * HD:(m + 1) * HD, :], w.expert2[:, e, :], h1[:, 2 + e, :],
                                                start=True, stop=True)
                    last.then_inc(pe_job, 1)
                    job(s, 13 + 2 * n, (11, 12)[n])
                    nc.tensor.matmul(bank[(0, 2)[n]][:, :], w.spread[:, n, :], coef_t[:, :], start=True, stop=True)\
                        .then_inc(pe_job, 1)

            def stage3(s):
                pe.wait_ge(dve_job, s * ND + (3 + AHEAD))
                for n, b in enumerate((3, 0)):
                    job(s, 16 + n, *((13, None), (None, 2))[n])
                    for m in range(2):
                        i = 2 * n + m
                        tok = slice(i * P, (i + 1) * P)
                        last = linear(bank[b][:, m * D:(m + 1) * D],
                                      [h2[:, 0, tok], h2[:, 1, tok], h2[:, 2, tok], coef_t[:, tok]],
                                      [w.down[:, 0, :], w.down[:, 1, :], w.down[:, 2, :], w.down_bias[:, :]])
                    last.then_inc(pe_job, 1)

            turn(0)
            turn(1)
            score(0, 0)
            over_tiles(core, pe, pair, idle, (idle, stage0, stage1, idle, stage2, idle, stage3, idle))

        @block.scalar
        def _(act):
            act.preload_act_table_set("exp_and_others")
            act.sem_inc(turned_ready, AHEAD)
            act.sem_inc(weight_ready, AHEAD)
            act.sem_inc(onehot_f_ready, AHEAD)
            act.sem_inc(act_job, AHEAD)

            def load_x(s):
                act.dma_start(xb[:, bass.ds(s % 2, 1), :, :].rearrange("p a i d -> p (a i) d"),
                              x_v[bass.ds(s, 1), :, :, :].rearrange("s p i d -> p (s i) d")).then_inc(x_loaded, 16)

            def widen(q, c):
                act.wait_ge(agg_done, 2 * q + (c - 1) + AHEAD)
                nc.scalar.activation(onehot_f[:, c, :].unsqueeze(1), onehot[:, bass.ds(q % 4, 1), c * P:(c + 1) * P], ACT.Copy)\
                    .then_inc(onehot_f_ready, 1)

            def take_turned(q):
                act.wait_ge(turned_psum, q + 1)
                act.wait_ge(score_psum, q - 1 + AHEAD)
                nc.scalar.activation(turned[:, bass.ds(q % 2, 1), :], turned_ps[:, bass.ds(q % 2, 1), :], ACT.Copy)\
                    .then_inc(turned_ready, 1)

            def weights(q):
                act.wait_ge(z_ready, q + 1 + AHEAD)
                act.wait_ge(weight_ready, q - 1 + AHEAD)
                nc.scalar.activation(th[:, bass.ds(q % 2, 1), :], z[:, bass.ds(q % 2, 1), :], ACT.Tanh, scale=0.5)\
                    .then_inc(tanh_own, 1)
                act.wait_ge(tanh_own, q + 1)
                act.wait_ge(agg_done, 2 * q - 2 + AHEAD)
                nc.scalar.activation(msg[:, bass.ds(q % 2, 1), :, HEADS * HD:MSG0].rearrange("p a c h -> p (a c) h"),
                                     th[:, bass.ds(q % 2, 1), :].rearrange("p a (c h) -> p (a c) h", c=2), ACT.Exp,
                                     bias=half[:, :], scale=0.5).then_inc(weight_ready, 1)

            def pair(q, t, i, first_of_tile, last_of_tile):
                widen(q, 0)
                take_turned(q + 2)
                widen(q, 1)
                weights(q + 1)

            def take(s, job, out, src, func, bias=0.0):
                act.wait_ge(pe_job, NJ * s + job + FAR)
                nc.scalar.activation(out, src, func, **({} if func == ACT.Copy else {"bias": bias})).then_inc(act_job, 1)

            def relu1(s, n, b):
                take(s, 4 + n, h1[:, n, :], bank[b][:, :], ACT.Relu, w.up1_bias[:, n:n + 1])

            def load_and_store(s):
                if not (isinstance(s, int) and s == 0):
                    act.wait_ge(dense_done, s + AHEAD)
                    store(s - 1)
                if not (isinstance(s, int) and s == ST - 1):
                    act.wait_ge(x_loaded, s * 16 + 16)
                    load_x(s + 1)

            def stage0(s):
                for b in range(2):
                    take(s, 1 + b, xt[:, b, :], bank[b][:, :], ACT.Copy)
                relu1(s, 0, 3)
                relu1(s, 1, 0)

            def gate_exp(s, n):
                act.wait_ge(gate_ready, s * 3 + n + AHEAD)
                nc.scalar.activation(gate[:, 2, :, :], gate[:, 1, :, :], ACT.Exp).then_inc(act_job, 1)

            def stage1(s):
                gate_exp(s, 1)
                relu1(s, 2, 1)
                relu1(s, 3, 2)
                gate_exp(s, 2)
                relu1(s, 4, 3)
                relu1(s, 5, 0)

            def stage2(s):
                take(s, 10, coef_t[:, :], bank[1][0:EXPERTS + 1, :], ACT.Copy)
                take(s, 11, h2[:, 0, :], bank[2][:, :], ACT.Relu, w.up2_bias[:, :])
                for n in range(2):
                    take(s, 12 + 2 * n, h2[:, 1 + n, :], bank[(3, 1)[n]][:, :], ACT.Relu, w.expert2_bias[:, n:n + 1])

            def store(s):
                act.dma_start(tab1_v[bass.ds(s, 1), :, :, :].rearrange("s p i d -> p (s i) d"), xn2[:, :, :]).then_inc(stored, 16)

            load_x(0)
            take_turned(0)
            take_turned(1)
            act.wait_ge(xn_ready, AHEAD)
            weights(0)
            over_tiles(core, act, pair, idle, (load_and_store, stage0, stage1, idle, stage2, idle, idle, idle))
            act.wait_ge(dense_done, ST + AHEAD)
            store(ST - 1)
            act.wait_ge(stored, 16 * ST)


def layer1(core, w):
    nc, io = core.nc, core.io
    with ExitStack() as ctx:
        sem = lambda n: core.sem(ctx, n)
        core.rounds = sem("rounds1")
        gathered = [sem(f"gathered1_{k}") for k in range(RING)]
        loaded, turned, turn_psum, ring_ones = sem("loaded1"), sem("turned1"), sem("turn_psum1"), sem("ring_ones")
        idx_ready, landed, onehot_ready, agg_done, agg_free = sem("idx_ready1"), sem("landed1"), sem("onehot_ready1"), sem("agg_done1"), sem("agg_free1")
        dve_tile, dve_dense, pe_job, act_job, dve_job = sem("dve_tile1"), sem("dve_dense1"), sem("pe_job1"), sem("act_job1"), sem("dve_job1")
        xn_ready, base_ready, stored, no_node_ready = sem("xn_ready1"), sem("base_ready1"), sem("stored1"), sem("no_node_ready")

        idx = core.sb("idx1", [P, SLOTS], U32, ctx)
        ring = core.sb("ring1", [P, SLOTS, D + 1], ctx=ctx)
        onehot = core.sb("onehot1", [P, 2, P], ctx=ctx)
        agg = core.sb("agg1", [P, QUAD, D], ctx=ctx)
        deg = core.sb("deg", [P, 1], ctx=ctx)
        no_node = core.sb("no_node", [P, T], ctx=ctx)
        nan_if_empty = core.sb("nan_if_empty", [P, 2, QUAD], ctx=ctx)
        stats = core.sb("stats1", [P, QUAD, 6], ctx=ctx)
        mv = core.sb("mv1", [P, QUAD, 2], ctx=ctx)
        var = core.sb("var1", [P, QUAD], ctx=ctx)
        rstd = core.sb("rstd1", [P, QUAD], ctx=ctx)
        rtmp = core.sb("rtmp1", [P, QUAD], ctx=ctx)
        x3 = core.sb("x3", [P, QUAD, D], ctx=ctx)
        xn = core.sb("xn1", [P, QUAD, D], ctx=ctx)
        base = core.sb("base1", [P, QUAD, D], ctx=ctx)
        xt = core.sb("xt1", [P, 2, TOK], ctx=ctx)
        h = core.sb("h", [P, BLK, TOK], ctx=ctx)
        w_gnn = h[:, 0, :].rearrange("p (b k) -> p b k", b=2)
        w_gnn_t = core.sb("w_gnn_t", [P, 2, D], ctx=ctx)
        w_gnn_bias = core.sb("w_gnn_bias", [P, D], ctx=ctx)
        w_up = core.sb("w_up", [P, 2, HID], ctx=ctx)
        w_up_bias = core.sb("w_up_bias", [P, BLK], ctx=ctx)
        w_down = core.sb("w_dn", [P, BLK, D], ctx=ctx)
        w_down_bias = core.sb("w_dn_bias", [1, D], ctx=ctx)
        w_route = core.sb("w_route", [P, D], ctx=ctx)
        w_route_bias = core.sb("w_route_bias", [P, 1], ctx=ctx)
        agg_ps = core.ps(ctx, "agg_ps1", [P, 2, 512])
        bank = [core.ps(ctx, f"bank1_{b}", [P, 512]) for b in range(4)]
        block = ctx.enter_context(nc.Block())
        base3_v = core.base3.rearrange("(s i p) d -> s p i d", i=QUAD, p=P)
        g = lambda n: io["L1_" + n]
        NJ, NA, ND = 16, 12, 4
        loads = [
            (w_gnn, g("gnn_W").rearrange("(b p) k -> p b k", p=P)),
            (w_gnn_bias[:, :], g("gnn_b").partition_broadcast(P)),
            (w_up[:, :, :], g("ffn_w1").rearrange("(k p) n -> p k n", p=P)),
            (w_up_bias[:, :], g("ffn_b1").rearrange("(b p) -> p b", p=P)),
            (w_down[:, :, :], g("ffn_w2").rearrange("(b p) d -> p b d", p=P)),
            (w_down_bias[:, :], g("ffn_b2").rearrange("(a n) -> a n", a=1)),
            (w_route[:, :], g("ffn_wr").rearrange("d o -> (o d)").partition_broadcast(P)),
            (w_route_bias[:, :], g("ffn_br").partition_broadcast(P)),
        ]

        @block.sync
        def _(sp):
            for dst, src in loads:
                sp.dma_start(dst, src, allow_slow_non_contiguous=True).then_inc(loaded, 16)
            relay_rounds(core, sp, gathered, landed)

        @block.gpsimd
        def _(pool):
            nc.gpsimd.memset(ring[:, :, D:D + 1], 1.0).then_inc(ring_ones, 1)
            nc.gpsimd.memset(no_node[:, :], 0.0).then_inc(no_node_ready, 1)
            pool.wait_ge(no_node_ready, 1)
            nc.gpsimd.affine_select(out=no_node[:, :], in_=no_node[:, :], compare_op=ALU.is_gt, fill=1.0, base=N,
                                    pattern=[[-P, T]], channel_multiplier=-1).then_inc(no_node_ready, 1)
            gather_rounds(core, pool, idx_ready, agg_done, lambda q: 2 * q + (2 - 2 * RING + FAR), gathered, core.tab1, D, idx, ring)

        @block.vector
        def _(dve):
            TILE = 4
            dve.sem_inc(dve_job, AHEAD)
            dve.sem_inc(agg_free, AHEAD)
            dve.sem_inc(base_ready, AHEAD)
            dve.sem_inc(onehot_ready, AHEAD)

            def indices(q):
                dve.tensor_copy(idx[:, bass.ds((q % RING) * 2, 2)], core.recs[:, bass.ds(q * 2, 2), 2].bitcast(I32))\
                    .then_inc(idx_ready, 1)

            def pair(q, t, i, first_of_tile, last_of_tile):
                for c in range(2):
                    dve.wait_ge(agg_done, 2 * q + (c - 1) + FAR)
                    dve.tensor_scalar(onehot[:, c, :], core.iota_f[:, :], core.recs[:, bass.ds(q * 2 + c, 1), 0],
                                      core.recs[:, bass.ds(q * 2 + c, 1), 1], ALU.is_equal, ALU.mult).then_inc(onehot_ready, 1)
                dve.wait_ge(landed, q + 1)
                indices(q + RING)

            def tile_end(t, i, s, q_end):
                ch = Chain(dve, dve_tile, t * TILE)
                a = agg_ps[:, i % 2, :]
                dve.wait_ge(agg_done, 2 * q_end + FAR)
                if not (isinstance(t, int) and t == 0):
                    ch.wait()
                ch.link(dve.tensor_tensor(deg[:, :], a[:, D:D + 1], no_node[:, bass.ds(t, 1)], ALU.add))
                ch.link(dve.reciprocal(deg[:, :], deg[:, :]))
                ch.step(dve.tensor_scalar(nan_if_empty[:, bass.ds(s % 2, 1), i], deg[:, :], 0.0, None, ALU.mult))
                if i == 0:
                    dve.wait_ge(pe_job, NJ * s - NJ + 2 + FAR)
                ch.step(dve.tensor_scalar(agg[:, i, :], a[:, 0:D], deg[:, :], None, ALU.mult))
                ch.wait()
                dve.sem_inc(agg_free, 1)
                assert ch.n == TILE

            for q in range(RING):
                indices(q)
            dve.wait_ge(loaded, 16 * len(loads))
            dve.wait_ge(no_node_ready, 2)

            S0, S2, S3 = 6 + 1 + 9 + 1 + 12 + 4, 1 + 4 + 2, 4
            S = S0 + S2 + S3

            def stage0(s):
                ch = Chain(dve, dve_dense, s * S)
                if not (isinstance(s, int) and s == 0):
                    ch.wait()
                rows = core.rows[:, bass.ds(s * QUAD, QUAD), :]
                for n, b in enumerate((2, 3)):
                    o = x3[:, 2 * n:2 * n + 2, :]
                    dve.wait_ge(pe_job, NJ * s + 3 + n + FAR)
                    ch.link(dve.tensor_tensor(o, bank[b][:, :].rearrange("p (i d) -> p i d", i=2),
                                              w_gnn_bias[:, :].unsqueeze(1).broadcast_to([P, 2, D]), ALU.add))
                    dve.sem_inc(dve_job, 1)
                    for i in range(2 * n, 2 * n + 2):
                        ch.step(dve.tensor_scalar(x3[:, i, :].unsqueeze(1), x3[:, i, :].unsqueeze(1), 0.0,
                                                  nan_if_empty[:, bass.ds(s % 2, 1), i], ALU.max, ALU.add))
                    ch.wait()
                ch.link(dve.tensor_tensor(x3[:, :, :], x3[:, :, :], rows, ALU.add))
                for i in range(QUAD):
                    ch.step(dve.bn_stats(stats[:, i, :], x3[:, i, :]))
                ch.wait_apart()
                for i in range(QUAD):
                    ch.step(dve.bn_aggr(mv[:, i, :], stats[:, i, :]))
                ch.wait()
                ch.link(dve.tensor_copy(var[:, :], mv[:, :, 1]))
                rstd_steps(dve, ch, var[:, :], rstd[:, :], rtmp[:, :])
                dve.wait_ge(pe_job, NJ * s - NJ + 6 + FAR)
                for i in range(QUAD):
                    ch.step(dve.tensor_scalar(xn[:, i, :], x3[:, i, :], mv[:, i, 0:1], rstd[:, i:i + 1],
                                              ALU.subtract, ALU.mult))
                ch.wait()
                dve.sem_inc(xn_ready, 1)
                assert ch.n == S0, ch.n

            def stage2(s):
                ch = Chain(dve, dve_dense, s * S + S0)
                ch.wait()
                if not (isinstance(s, int) and s == 0):
                    dve.wait_ge(stored, s * 16)
                ch.link(dve.tensor_tensor(base[:, :, :], x3[:, :, :], xn[:, :, :], ALU.add))
                dve.sem_inc(base_ready, 1)
                for i in range(QUAD):
                    ch.step(dve.tensor_tensor(x3[:, i, :], xn[:, i, :], w_route[:, :], ALU.mult))
                ch.wait()
                ch.link(dve.tensor_reduce(core.score[:, bass.ds(s * QUAD, QUAD)], x3[:, :, :], mybir.AxisListType.X, ALU.add))
                ch.step(dve.tensor_scalar(core.score[:, bass.ds(s * QUAD, QUAD)], core.score[:, bass.ds(s * QUAD, QUAD)],
                                          w_route_bias[:, :], None, ALU.add))
                assert ch.n == S2, ch.n

            def stage3(s):
                ch = Chain(dve, dve_dense, s * S + S0 + S2)
                ch.wait()
                for i in range(QUAD):
                    if i % 2 == 0:
                        dve.wait_ge(pe_job, NJ * s + 15 + i // 2 + FAR)
                    ch.step(dve.tensor_scalar(core.rows[:, bass.ds(s * QUAD + i, 1), :],
                                              bank[2 + i // 2][:, (i % 2) * D:(i % 2 + 1) * D].unsqueeze(1),
                                              core.score[:, bass.ds(s * QUAD + i, 1)], None, ALU.mult))
                    if i % 2:
                        ch.wait()
                        dve.sem_inc(dve_job, 1)
                assert ch.n == S3

            over_tiles(core, dve, pair, tile_end, (idle, stage0, idle, idle, stage2, idle, idle, stage3))

        @block.tensor
        def _(pe):
            pe.sem_inc(agg_done, FAR)
            pe.sem_inc(pe_job, FAR)
            pe.wait_ge(loaded, 16 * len(loads))
            for kb in range(2):
                for ob in range(2):
                    last = nc.tensor.transpose(bank[0][:, kb * D + ob * P:kb * D + (ob + 1) * P], w_gnn[:, ob, kb * P:(kb + 1) * P],
                                               core.ident_f[:, :])
            last.then_inc(turn_psum, 1)
            pe.wait_ge(turned, 1)
            pe.wait_ge(ring_ones, 1)

            def pair(q, t, i, first_of_tile, last_of_tile):
                out = agg_ps[:, i % 2, 0:D + 1]
                if first_of_tile:
                    pe.wait_ge(agg_free, t - 1 + AHEAD)
                    nc.tensor.matmul(out, core.zero_b[:, 0:P], core.zero_b[:, P - 1:P + D], start=True, stop=False,
                                     skip_group_check=True)
                pe.wait_ge(landed, q + 1)
                for c in range(2):
                    pe.wait_ge(onehot_ready, 2 * q + (c + 1) + AHEAD)
                    last = nc.tensor.matmul(out, onehot[:, c, :],
                                            ring[:, bass.ds((q % RING) * 2 + c, 1), :].rearrange("p a d -> p (a d)"),
                                            start=False, stop=last_of_tile and c == 1, skip_group_check=True)
                    last.then_inc(agg_done, 1)

            def linear(out, w_blocks, x_blocks, more=()):
                pairs = [*zip(w_blocks, x_blocks), *more]
                for n, (a, b) in enumerate(pairs):
                    last = nc.tensor.matmul(out, a, b, start=(n == 0), stop=(n == len(pairs) - 1))
                return last

            def job(s, act=None, dve=None):
                if act is not None:
                    pe.wait_ge(act_job, s * NA + (act + AHEAD))
                if dve is not None:
                    pe.wait_ge(dve_job, s * ND + (dve + AHEAD))

            def turn4(b, src):
                for i in range(QUAD):
                    last = nc.tensor.transpose(bank[b][:, i * P:(i + 1) * P], src(i), core.ident_f[:, :])
                last.then_inc(pe_job, 1)

            def stage0(s):
                pe.wait_ge(agg_free, s * QUAD + QUAD + AHEAD)
                for b in range(2):
                    job(s, (-2, -1)[b])
                    turn4(b, lambda i: agg[:, i, b * P:(b + 1) * P])
                for n in range(2):
                    job(s, 2, (-1, 0)[n])
                    for m in range(2):
                        i = 2 * n + m
                        last = linear(bank[2 + n][:, m * D:(m + 1) * D], [xt[:, k, i * P:(i + 1) * P] for k in range(2)],
                                      [w_gnn_t[:, k, :] for k in range(2)])
                    last.then_inc(pe_job, 1)

            def up(s, b, act=None, dve=None):
                job(s, act, dve)
                n = up.n
                up.n = (n + 1) % BLK
                linear(bank[(2 + n) % 4][:, :], [w_up[:, k, n * P:(n + 1) * P] for k in range(2)],
                       [xt[:, k, :] for k in range(2)]).then_inc(pe_job, 1)
            up.n = 0

            def stage1(s):
                pe.wait_ge(xn_ready, s + 1)
                for b in range(2):
                    job(s, 1 + b)
                    turn4(b, lambda i: xn[:, i, b * P:(b + 1) * P])
                job(s, 4)
                up(s, 2, None, 1)
                up(s, 3, None, 2)
                up(s, 0, 3)
                up(s, 1, 4)

            def stage2(s):
                for n in range(4):
                    up(s, (2 + n) % 4, 5 + n)

            def stage3(s):
                for n in range(2):
                    job(s, 12)
                    for m in range(2):
                        i = 2 * n + m
                        last = linear(bank[2 + n][:, m * D:(m + 1) * D], [h[:, k, i * P:(i + 1) * P] for k in range(BLK)],
                                      [w_down[:, k, :] for k in range(BLK)], [(core.ones_f[0:1, :], w_down_bias[:, :])])
                    last.then_inc(pe_job, 1)

            over_tiles(core, pe, pair, idle, (stage0, idle, idle, stage1, stage2, idle, stage3, idle))

        @block.scalar
        def _(act):
            act.wait_ge(turn_psum, 1)
            nc.scalar.activation(flat(w_gnn_t[:, :, :]), bank[0][:, :], ACT.Copy).then_inc(turned, 1)
            act.preload_act_table_set(GELU_SET)
            act.sem_inc(act_job, AHEAD)

            def take(s, job, out, src, func, **kw):
                act.wait_ge(pe_job, NJ * s + job + FAR)
                nc.scalar.activation(out, src, func, **kw).then_inc(act_job, 1)

            def stage0(s):
                for b in range(2):
                    take(s, 1 + b, xt[:, b, :], bank[b][:, :], ACT.Copy)

            def gelu(s, n):
                take(s, 7 + n, h[:, n, :], bank[(2 + n) % 4][:, :], ACT.Gelu_apprx_tanh, bias=w_up_bias[:, n:n + 1])

            def stage1(s):
                for b in range(2):
                    take(s, 5 + b, xt[:, b, :], bank[b][:, :], ACT.Copy)
                for n in range(4):
                    gelu(s, n)

            def stage2(s):
                for n in range(4, BLK):
                    gelu(s, n)
                act.wait_ge(base_ready, s + 1 + AHEAD)
                act.dma_start(base3_v[bass.ds(s, 1), :, :, :].rearrange("s p i d -> p (s i) d"), base[:, :, :]).then_inc(stored, 16)

            over_tiles(core, act, idle, idle, (stage0, idle, idle, stage1, stage2, idle, idle, idle))
            act.wait_ge(stored, 16 * ST)


GELU_SET = "gelu_apprx_tanh_and_others"


def select(core, w):
    nc, io = core.nc, core.io
    with ExitStack() as ctx:
        sem = lambda n: core.sem(ctx, n)
        own, count_ready, total_psum, valid_ready = sem("own5"), sem("count_ready5"), sem("total_psum5"), sem("valid_ready5")
        equal_ready, order_psum = sem("equal_ready5"), sem("order_psum5")
        base_loaded = [sem(f"base_loaded{k}") for k in range(2)]
        out_stored = [sem(f"out_stored{k}") for k in range(2)]
        out_ready = sem("out_ready5")

        key = core.sb("key5", [P, T], I32, ctx)
        sign = core.sb("sign5", [P, T], I32, ctx)
        half_i = core.sb("half_i5", [P, T], I32, ctx)
        hi = core.sb("hi5", [P, T], ctx=ctx)
        lo = core.sb("lo5", [P, T], ctx=ctx)
        valid = core.sb("valid5", [P, T], ctx=ctx)
        node = core.sb("node5", [P, T], I32, ctx)
        hit = core.sb("hit5", [P, T], ctx=ctx)
        mask = core.sb("mask5", [P, T], ctx=ctx)
        level = core.sb("level5", [P, 1], ctx=ctx)
        tried = core.sb("tried5", [P, 1], ctx=ctx)
        count = core.sb("count5", [P, 1], ctx=ctx)
        grow = core.sb("grow5", [P, 1], ctx=ctx)
        want = core.sb("want5", [P, 1], ctx=ctx)
        equal = core.sb("equal5", [P, T], ctx=ctx)
        equal_b = core.sb("equal_b5", [P, T], BF16, ctx)
        above = core.sb("above5", [P, T + 1], ctx=ctx)
        zeros = core.sb("zeros5", [P, T], ctx=ctx)
        base = core.sb("base5", [P, 2, QUAD, D], ctx=ctx)
        total_ps = core.ps(ctx, "total_ps5", [P, 512])
        order_ps = core.ps(ctx, "order_ps5", [P, 512])
        column_ps = core.ps(ctx, "column_ps5", [P, 512])
        block = ctx.enter_context(nc.Block())
        base3_v = core.base3.rearrange("(s i p) d -> s p i d", i=QUAD, p=P)
        out_v = io["out"].rearrange("(s i p) d -> s p i d", i=QUAD, p=P)

        @block.sync
        def _(sp):
            for s in range(ST):
                if s >= 2:
                    sp.wait_ge(out_stored[s % 2], 16 * (s // 2))
                sp.dma_start(base[:, s % 2, :, :], base3_v[s, :, :, :]).then_inc(base_loaded[s % 2], 16)

        @block.gpsimd
        def _(pool):
            nc.gpsimd.iota(node[:, :], [[P, T]], base=0, channel_multiplier=1).then_inc(valid_ready, 1)

        @block.vector
        def _(dve):
            ch = Chain(dve, own)
            ch.step(dve.memset(zeros[:, :], 0.0))
            ch.step(dve.memset(level[:, :], 0.0))
            ch.step(dve.memset(want[:, :], float(CAPACITY)))
            dve.wait_ge(valid_ready, 1)
            ch.step(dve.tensor_scalar(valid[:, :], node[:, :], float(N), None, ALU.is_lt))
            bits = core.score[:, :].bitcast(I32)
            ch.link(dve.tensor_scalar(sign[:, :], bits, 31, None, ALU.arith_shift_right))
            ch.link(dve.tensor_scalar(sign[:, :], sign[:, :], -(1 << 31), None, ALU.bitwise_or))
            ch.link(dve.tensor_tensor(key[:, :], bits, sign[:, :], ALU.bitwise_xor))
            ch.link(dve.tensor_scalar(half_i[:, :], key[:, :], 16, None, ALU.logical_shift_right))
            ch.link(dve.tensor_tensor(hi[:, :], half_i[:, :], valid[:, :], ALU.mult))
            ch.link(dve.tensor_scalar(half_i[:, :], key[:, :], 0xFFFF, None, ALU.bitwise_and))
            ch.link(dve.tensor_tensor(lo[:, :], half_i[:, :], valid[:, :], ALU.mult))
            ch.link(dve.tensor_tensor(hit[:, :], core.score[:, :], core.score[:, :], ALU.not_equal))
            ch.step(dve.scalar_tensor_tensor(hi[:, :], hit[:, :], 65535.0, hi[:, :], ALU.mult, ALU.max))
            ch.link(dve.scalar_tensor_tensor(lo[:, :], hit[:, :], 65535.0, lo[:, :], ALU.mult, ALU.max))
            counts = 0

            def total():
                nonlocal counts
                counts += 1
                dve.sem_inc(count_ready, 1)
                dve.wait_ge(total_psum, counts)
                return total_ps[:, 0:1]

            def descend(vals):
                for b in range(15, -1, -1):
                    ch.link(dve.tensor_scalar(tried[:, :], level[:, :], float(1 << b), None, ALU.add))
                    ch.link(dve.tensor_scalar(hit[:, :], vals, tried[:, :], None, ALU.is_ge, ALU.add, accum_out=count[:, :]))
                    ch.link(dve.tensor_scalar(grow[:, :], total(), want[:, :], float(1 << b), ALU.is_ge, ALU.mult))
                    ch.link(dve.tensor_tensor(level[:, :], level[:, :], grow[:, :], ALU.add))

            descend(hi[:, :])
            ch.link(dve.tensor_scalar(mask[:, :], hi[:, :], level[:, :], None, ALU.is_gt, ALU.add, accum_out=count[:, :]))
            ch.step(dve.tensor_tensor(want[:, :], want[:, :], total(), ALU.subtract))
            ch.step(dve.tensor_scalar(equal[:, :], hi[:, :], level[:, :], None, ALU.is_equal))
            ch.link(dve.tensor_scalar(lo[:, :], lo[:, :], 1.0, None, ALU.add))
            ch.link(dve.tensor_tensor(lo[:, :], lo[:, :], equal[:, :], ALU.mult))
            ch.link(dve.memset(level[:, :], 1.0))
            descend(lo[:, :])
            ch.link(dve.tensor_scalar(hit[:, :], lo[:, :], level[:, :], None, ALU.is_gt, ALU.add, accum_out=count[:, :]))
            ch.step(dve.tensor_tensor(want[:, :], want[:, :], total(), ALU.subtract))
            ch.step(dve.tensor_tensor(mask[:, :], mask[:, :], hit[:, :], ALU.add))
            ch.link(dve.tensor_scalar(equal[:, :], lo[:, :], level[:, :], None, ALU.is_equal))
            ch.link(dve.tensor_copy(equal_b[:, :], equal[:, :]))
            dve.sem_inc(equal_ready, 1)
            dve.wait_ge(order_psum, 1)
            ch.link(dve.memset(above[:, :], 0.0))
            ch.link(dve.tensor_tensor_scan(above[:, 1:T + 1], column_ps[:, 0:T], zeros[:, :], 0.0, ALU.add, ALU.add))
            ch.link(dve.tensor_tensor(above[:, 0:T], above[:, 0:T], order_ps[:, 0:T], ALU.add))
            ch.link(dve.tensor_scalar(above[:, 0:T], above[:, 0:T], want[:, :], None, ALU.is_lt))
            ch.link(dve.tensor_tensor(equal[:, :], equal[:, :], above[:, 0:T], ALU.mult))
            ch.link(dve.tensor_tensor(mask[:, :], mask[:, :], equal[:, :], ALU.add))
            for s in range(ST):
                dve.wait_ge(base_loaded[s % 2], 16 * (s // 2 + 1))
                for i in range(QUAD):
                    t = s * QUAD + i
                    o = base[:, s % 2, i, :]
                    dve.scalar_tensor_tensor(o, core.rows[:, t, :], mask[:, t:t + 1], o, ALU.mult, ALU.add).then_inc(out_ready, 1)

        @block.tensor
        def _(pe):
            for n in range(2 * 16 + 2):
                pe.wait_ge(count_ready, n + 1)
                nc.tensor.matmul(total_ps[:, 0:1], core.ones_f[:, :], count[:, :], start=True, stop=True).then_inc(total_psum, 1)
            pe.wait_ge(equal_ready, 1)
            nc.tensor.matmul(column_ps[:, 0:T], core.ones_f[:, :], equal[:, :], start=True, stop=True)
            nc.tensor.matmul(order_ps[:, 0:T], core.before[:, :], equal_b[:, :], start=True, stop=True).then_inc(order_psum, 1)

        @block.scalar
        def _(act):
            for s in range(ST):
                act.wait_ge(out_ready, QUAD * (s + 1))
                act.dma_start(out_v[s, :, :, :], base[:, s % 2, :, :]).then_inc(out_stored[s % 2], 16)
            for k in range(2):
                act.wait_ge(out_stored[k], 16 * ((ST + 1 - k) // 2))


def program(nc, **io):
    with ExitStack() as ctx:
        core = Core(nc, ctx, io)
        core.edges = Edges(core)
        with ExitStack() as layer0_only:
            core.ctx = layer0_only
            w = Weights(core)
            core.ctx = ctx
            setup(core, w)
            bucket(core, w)
            layer0(core, w)
        layer1(core, None)
        select(core, None)


_PLAIN = ["L0_gnn_W_lin", "L0_gnn_b_lin", "L0_gnn_att_w", "L0_gnn_att_b", "L0_gnn_emb_w", "L0_gnn_emb_b",
          "L0_ffn_sW1", "L0_ffn_sb1", "L0_ffn_sW2", "L0_ffn_sb2", "L0_ffn_sW3", "L0_ffn_sb3",
          "L0_ffn_eW1", "L0_ffn_eb1", "L0_ffn_eW2", "L0_ffn_eb2", "L0_ffn_eW3", "L0_ffn_eb3", "L0_ffn_gW", "L0_ffn_gb",
          "L1_gnn_W", "L1_gnn_b", "L1_ffn_wr", "L1_ffn_br", "L1_ffn_w1", "L1_ffn_b1", "L1_ffn_w2", "L1_ffn_b2"]


def kernel(**inputs):
    import numpy as _np
    import concourse.bacc as _bacc
    from concourse import mybir as _mybir
    from concourse.bass_utils import run_bass_kernel_spmd as _run

    pad = P * EJ - E
    arrays = {
        "x": _np.pad(_np.asarray(inputs["x"]), ((0, NP - N), (0, 0))),
        "src": _np.pad(_np.asarray(inputs["src"]), (0, pad), constant_values=PAD_SRC).reshape(P, EJ),
        "dst": _np.pad(_np.asarray(inputs["dst"]), (0, pad)).reshape(P, EJ),
        "edge_weight": _np.pad(_np.asarray(inputs["edge_weight"]), (0, pad)).reshape(P, EJ),
    }
    for name in _PLAIN:
        arrays[name] = _np.ascontiguousarray(inputs[name])
    nc = _bacc.Bacc("TRN2", target_bir_lowering=False, num_devices=1)
    io = {n: nc.dram_tensor(f"in_{n}", a.shape, _mybir.dt.from_np(a.dtype), kind="ExternalInput").ap()
          for n, a in arrays.items()}
    io["out"] = nc.dram_tensor("out_rows", (NP, D), F32, kind="ExternalOutput").ap()
    program(nc, **io)
    r = _run(nc, [{f"in_{n}": a for n, a in arrays.items()}], core_ids=[0])
    return r.results[0]["out_rows"][:N]
```
